# Optimizing a Trainium2 kernel written in Bass

```python
import numpy as np
import jax
import jax.numpy as jnp

def _softmax(x, axis=-1):
    return jax.nn.softmax(x, axis=axis)

def _gelu(x):
    return jax.nn.gelu(x, approximate=True)

def _silu(x):
    return jax.nn.silu(x)

def _sigmoid(x):
    return jax.nn.sigmoid(x)

def _layernorm(x, axis=-1, eps=1e-05):
    m = jnp.mean(x, axis=axis, keepdims=True)
    v = jnp.var(x, axis=axis, keepdims=True)
    return (x - m) / jnp.sqrt(v + eps)

def _scatter_add(tgt, idx, src, axis=0):
    return tgt.at[idx].add(src)

def _segment_sum(src, seg, n):
    return jax.ops.segment_sum(src, seg, n)
kernel_name = 'mk_flamingo_gated_d1_seqx_r8_d10e80'

def setup_inputs(seed: int=0):
    np.random.seed(seed)
    _w = jnp.asarray

    def _rec_inputs():
        import jax
        import jax.numpy as jnp
        _rk = jax.random.key(seed)
        x = -0.0005207 + 1.001 * jax.random.normal(jax.random.fold_in(_rk, 1), (32, 64, 512), jnp.float32)
        _lenS = 64 - jax.random.randint(jax.random.fold_in(_rk, 7), (32,), 0, max(1, 64 // 4) + 1, jnp.int32)
        _lenS2 = 64 - jax.random.randint(jax.random.fold_in(_rk, 8), (32,), 0, max(1, 64 // 4) + 1, jnp.int32)
        _ctx_4096P = jax.random.normal(jax.random.fold_in(_rk, 11), (32, 16, 512), jnp.float32)
        _ctx_4096c = jax.random.dirichlet(jax.random.fold_in(_rk, 511), 0.3 * jnp.ones((16,), jnp.float32), (32, 64))
        _ctx_4096t = jnp.einsum('bsk,bkd->bsd', _ctx_4096c, _ctx_4096P)
        _ctx_4096t = _ctx_4096t * jax.lax.rsqrt(jnp.mean(jnp.square(_ctx_4096t)) + 1e-12) * 0.953939
        ctx_4096 = -0.00010331 + 0.999899 * (_ctx_4096t + 0.3 * jax.random.normal(jax.random.fold_in(_rk, 611), (32, 64, 512), jnp.float32))
        _g = jax.random.normal(jax.random.fold_in(_rk, 9001), (2, 1), jnp.float32)
        _g = jnp.sign(_g) * jnp.maximum(jnp.abs(_g), 1.0) + (_g == 0) * 1.0
        g_xattn = _g[0]
        g_ffn = _g[1]
        return (x, ctx_4096, g_xattn, g_ffn)
    x, ctx_4096, g_xattn, g_ffn = _rec_inputs()

    def _L0_xattn_setup():
        import jax, jax.numpy as jnp
        import numpy as np
        HEADS = 32
        KV_HEADS = 8
        HEAD_DIM = 128
        EPS = 1e-06

        def rms_norm(x, w):
            var = jnp.mean(jnp.square(x.astype(jnp.float32)), axis=-1, keepdims=True)
            return (x.astype(jnp.float32) * jax.lax.rsqrt(var + EPS)).astype(x.dtype) * w
        key = jax.random.key(seed)
        ks = jax.random.split(key, 6)
        bsz, n_lat, seq, hidden = (8, 64, 512, 512)
        return {'latents': jax.random.normal(ks[0], (bsz, n_lat, hidden), jnp.float32), 'context': jax.random.normal(ks[1], (bsz, seq, hidden), jnp.float32), 'Wq': jax.random.normal(ks[2], (hidden, HEADS * HEAD_DIM), jnp.float32) * 0.02, 'Wk': jax.random.normal(ks[3], (hidden, KV_HEADS * HEAD_DIM), jnp.float32) * 0.02, 'Wv': jax.random.normal(ks[4], (hidden, KV_HEADS * HEAD_DIM), jnp.float32) * 0.02, 'Wo': jax.random.normal(ks[5], (HEADS * HEAD_DIM, hidden), jnp.float32) * 0.02, 'q_norm_w': jnp.ones((HEAD_DIM,), jnp.float32), 'k_norm_w': jnp.ones((HEAD_DIM,), jnp.float32)}
    _L0_xattn_all = _L0_xattn_setup()
    _L0_xattn_in = {k: v for k, v in _L0_xattn_all.items() if k in ('Wq', 'Wk', 'Wv', 'Wo', 'q_norm_w', 'k_norm_w')}
    del _L0_xattn_all

    def _L0_ffn_setup():
        import jax, jax.numpy as jnp
        import numpy as np
        B, S, D = (4, 256, 512)
        NUM_EXPERTS, TOP_K = (3, 2)

        def _expert_outputs(h, w1, b1, w2, b2):
            pre = jnp.einsum('bsd,edf->ebsf', h, w1) + b1[:, None, None, :]
            act = jnp.stack([jnp.tanh(pre[0]), jax.nn.gelu(pre[1], approximate=False), jax.nn.silu(pre[2])])
            return jnp.einsum('ebsf,efd->ebsd', act, w2) + b2[:, None, None, :]
        key = jax.random.key(seed)
        ks = jax.random.split(key, 8)
        scale_in = 1.0 / np.sqrt(D)
        scale_gate = 1.0 / np.sqrt(D + 1)
        return {'h': jax.random.normal(ks[0], (B, S, D), dtype=jnp.float32), 'gate_w': jax.random.uniform(ks[1], (D + 1, NUM_EXPERTS), minval=-scale_gate, maxval=scale_gate, dtype=jnp.float32), 'gate_b': jnp.zeros((NUM_EXPERTS,), dtype=jnp.float32), 'w1': jax.random.uniform(ks[2], (NUM_EXPERTS, D, D), minval=-scale_in, maxval=scale_in, dtype=jnp.float32), 'b1': jnp.zeros((NUM_EXPERTS, D), dtype=jnp.float32), 'w2': jax.random.uniform(ks[3], (NUM_EXPERTS, D, D), minval=-scale_in, maxval=scale_in, dtype=jnp.float32), 'b2': jnp.zeros((NUM_EXPERTS, D), dtype=jnp.float32)}
    _L0_ffn_all = _L0_ffn_setup()
    _L0_ffn_in = {k: v for k, v in _L0_ffn_all.items() if k in ('gate_w', 'gate_b', 'w1', 'b1', 'w2', 'b2')}
    del _L0_ffn_all
    return {'x': x, 'ctx_4096': ctx_4096, 'g_xattn': g_xattn, 'g_ffn': g_ffn, 'L0_xattn_Wq': _L0_xattn_in['Wq'], 'L0_xattn_Wk': _L0_xattn_in['Wk'], 'L0_xattn_Wv': _L0_xattn_in['Wv'], 'L0_xattn_Wo': _L0_xattn_in['Wo'], 'L0_xattn_q_norm_w': _L0_xattn_in['q_norm_w'], 'L0_xattn_k_norm_w': _L0_xattn_in['k_norm_w'], 'L0_ffn_gate_w': _L0_ffn_in['gate_w'], 'L0_ffn_gate_b': _L0_ffn_in['gate_b'], 'L0_ffn_w1': _L0_ffn_in['w1'], 'L0_ffn_b1': _L0_ffn_in['b1'], 'L0_ffn_w2': _L0_ffn_in['w2'], 'L0_ffn_b2': _L0_ffn_in['b2']}

def reference(x, ctx_4096, g_xattn, g_ffn, L0_xattn_Wq, L0_xattn_Wk, L0_xattn_Wv, L0_xattn_Wo, L0_xattn_q_norm_w, L0_xattn_k_norm_w, L0_ffn_gate_w, L0_ffn_gate_b, L0_ffn_w1, L0_ffn_b1, L0_ffn_w2, L0_ffn_b2):
    import jax
    import jax.numpy as jnp

    def _L0_xattn_ref(latents, context, Wq, Wk, Wv, Wo, q_norm_w, k_norm_w):
        import jax, jax.numpy as jnp
        import numpy as np
        HEADS = 32
        KV_HEADS = 8
        HEAD_DIM = 128
        EPS = 1e-06

        def rms_norm(x, w):
            var = jnp.mean(jnp.square(x.astype(jnp.float32)), axis=-1, keepdims=True)
            return (x.astype(jnp.float32) * jax.lax.rsqrt(var + EPS)).astype(x.dtype) * w
        bsz, q_len, hidden = latents.shape
        kv = jnp.concatenate([context, latents], axis=1)
        kv_len = kv.shape[1]
        groups = HEADS // KV_HEADS
        q = (latents @ Wq).reshape(bsz, q_len, HEADS, HEAD_DIM).transpose(0, 2, 1, 3)
        k = (kv @ Wk).reshape(bsz, kv_len, KV_HEADS, HEAD_DIM).transpose(0, 2, 1, 3)
        v = (kv @ Wv).reshape(bsz, kv_len, KV_HEADS, HEAD_DIM).transpose(0, 2, 1, 3)
        q = rms_norm(q, q_norm_w)
        k = rms_norm(k, k_norm_w)
        qg = q.reshape(bsz, KV_HEADS, groups, q_len, HEAD_DIM)
        scale = 1.0 / np.sqrt(HEAD_DIM)
        scores = jnp.einsum('bhgqd,bhkd->bhgqk', qg, k) * scale
        probs = jax.nn.softmax(scores.astype(jnp.float32), axis=-1).astype(q.dtype)
        out = jnp.einsum('bhgqk,bhkd->bhgqd', probs, v)
        out = out.reshape(bsz, HEADS, q_len, HEAD_DIM).transpose(0, 2, 1, 3)
        out = out.reshape(bsz, q_len, HEADS * HEAD_DIM)
        return out @ Wo

    def _L0_ffn_ref(h, gate_w, gate_b, w1, b1, w2, b2):
        import jax, jax.numpy as jnp
        import numpy as np
        B, S, D = (4, 256, 512)
        NUM_EXPERTS, TOP_K = (3, 2)

        def _expert_outputs(h, w1, b1, w2, b2):
            pre = jnp.einsum('bsd,edf->ebsf', h, w1) + b1[:, None, None, :]
            act = jnp.stack([jnp.tanh(pre[0]), jax.nn.gelu(pre[1], approximate=False), jax.nn.silu(pre[2])])
            return jnp.einsum('ebsf,efd->ebsd', act, w2) + b2[:, None, None, :]
        b, s, d = h.shape
        vision_len = int(s * 0.3)
        text_strength = jnp.mean(jnp.abs(h[:, vision_len:, :]), axis=(1, 2), keepdims=True)
        vision_strength = jnp.mean(jnp.abs(h[:, :vision_len, :]), axis=(1, 2), keepdims=True)
        modality_ratio = text_strength / (vision_strength + 1e-08)
        modality_ratio = jnp.broadcast_to(modality_ratio, (b, s, 1))
        router_input = jnp.concatenate([h, modality_ratio], axis=-1)
        gate_logits = router_input @ gate_w + gate_b
        gate_scores = jax.nn.softmax(gate_logits, axis=-1)
        top_val, top_idx = jax.lax.top_k(gate_scores, TOP_K)
        top_val = top_val / (jnp.sum(top_val, axis=-1, keepdims=True) + 1e-08)
        expert_out = _expert_outputs(h, w1, b1, w2, b2)
        moe_out = jnp.zeros_like(h)
        batch_idx = jnp.arange(b)
        for i in range(TOP_K):
            j = top_idx[:, 0, i]
            out_i = expert_out[j, batch_idx]
            moe_out = moe_out + top_val[..., i:i + 1] * out_i
        return moe_out
    x = x + jnp.tanh(g_xattn[0]) * _L0_xattn_ref(_layernorm(x, axis=-1), ctx_4096, L0_xattn_Wq, L0_xattn_Wk, L0_xattn_Wv, L0_xattn_Wo, L0_xattn_q_norm_w, L0_xattn_k_norm_w)
    x = x + jnp.tanh(g_ffn[0]) * _L0_ffn_ref(_layernorm(x, axis=-1), L0_ffn_gate_w, L0_ffn_gate_b, L0_ffn_w1, L0_ffn_b1, L0_ffn_w2, L0_ffn_b2)
    return x

_drawn_inputs = setup_inputs


def setup_inputs(seed=0):
    import zlib

    import numpy as np

    out = dict(_drawn_inputs(seed))
    spreads = {'L0_xattn_q_norm_w': (1.0, 0.2),
     'L0_xattn_k_norm_w': (1.0, 0.2),
     'L0_ffn_gate_b': (0.0, 0.1),
     'L0_ffn_b1': (0.0, 0.321),
     'L0_ffn_b2': (0.0, 0.1)}
    factors = {}
    for name, (base, spread) in spreads.items():
        noise = np.random.default_rng([zlib.crc32(name.encode()), seed]).standard_normal(out[name].shape)
        drawn = base * np.exp(spread * noise) if base else spread * noise
        out[name] = jnp.asarray(drawn.astype(out[name].dtype))
    for name, factor in factors.items():
        out[name] = (out[name] * factor).astype(out[name].dtype)
    return out
```

```python
import concourse.bass as bass
from concourse import mybir
from contextlib import ExitStack

B, S, D = 32, 64, 512
HEADS, KVH, HD = 32, 8, 128
GRP = HEADS // KVH
NE = 3
P = 128
CH = D // P
NB = P // S
CELLS = 4
QUARTERS = B // (NB * CELLS)
ITS = KVH // 2
NIT = QUARTERS * ITS
STEPS = 2 * CELLS
NCELL = NIT * STEPS
PIECE = 512
PIECES = 10
RING = 5
WCOLS = PIECES * PIECE
SPLITS = [(0, 1, 2), (3, 4, 5), (6, 7), (8, 9)]
TILE = CH * NB * 2 * S
VIS = int(S * 0.3)
LN_EPS, RMS_EPS = 1e-5, 1e-6
FW = NE * CH * D
FPIECES = FW // PIECE
GT = P * CELLS
CHAIN = 35


def flamingo_block(nc, x, ctx_rows, g_xattn, g_ffn, wq, wk, wv, wo, qnw, knw, gate_w, gate_b, w1, b1, w2, b2, consts, x2_dram, out):
    fp32, f32r = mybir.dt.float32, mybir.dt.float32r
    ALU, ACT, AX = mybir.AluOpType, mybir.ActivationFunctionType, mybir.AxisListType

    x_rows = x.rearrange("b s d -> (b s) d").rearrange("(c p) d -> p c d", p=P)
    c_rows = ctx_rows.rearrange("b s d -> (b s) d").rearrange("(c p) d -> p c d", p=P)
    x2_rows = x2_dram.rearrange("(c p) d -> p c d", p=P)
    o_rows = out.rearrange("b s d -> (b s) d").rearrange("(c p) d -> p c d", p=P)
    wq_v = wq.rearrange("(c p) n -> p c n", p=P)
    wk_v = wk.rearrange("(c p) n -> p c n", p=P)
    wv_v = wv.rearrange("(c p) n -> p c n", p=P)
    wo_v = wo.rearrange("(h p) n -> p h n", p=P)
    w1_v = w1.rearrange("e (c p) n -> p (e c) n", p=P)
    w2_v = w2.rearrange("e (c p) n -> p (e c) n", p=P)

    es = ExitStack()
    with es:
        def sb(name, shape, dt=fp32):
            return es.enter_context(nc.sbuf_tensor(name, shape, dt))

        def sem(name):
            return es.enter_context(nc.semaphore(name))

        kvt_hi = sb("kvt_hi", [P, 2 * CELLS * TILE], f32r)
        kvt_lo = sb("kvt_lo", [P, 2 * CELLS * TILE], f32r)
        w_hi = sb("w_hi", [P, 2 * WCOLS], f32r)
        w_lo = sb("w_lo", [P, 2 * WCOLS], f32r)
        raw = sb("raw", [P, RING, PIECE])
        y = sb("y", [P, 2 * CELLS, D])
        work = sb("work", [P, 26 * HD])
        at = [0]

        def part(k):
            at[0] += k * HD
            return work[:, at[0] - k * HD:at[0]]

        qhat = part(2 * GRP).rearrange("p (k g d) -> p k g d", k=2, g=GRP)
        khat = part(NB).rearrange("p (b d) -> p b d", b=NB)
        qT = part(GRP).rearrange("p (b g s) -> p b g s", b=NB, g=GRP)
        kT = part(NB).rearrange("p (b k) -> p b k", b=NB)
        prob = part(GRP).rearrange("p (r k) -> p r k", r=GRP)
        sq = part(GRP).rearrange("p (g d) -> p g d", g=GRP)
        sqk = part(NB).rearrange("p (b d) -> p b d", b=NB)
        v_hi = sb("v_hi", [P, 2, NB, HD], f32r)
        v_lo = sb("v_lo", [P, 2, NB, HD], f32r)
        pT_hi = sb("pT_hi", [P, NB, GRP * S], f32r)
        pT_lo = sb("pT_lo", [P, NB, GRP * S], f32r)
        oT_hi = sb("oT_hi", [P, GRP, NB, S], f32r)
        oT_lo = sb("oT_lo", [P, GRP, NB, S], f32r)
        rows3 = sb("rows3", [P, 3 * D])
        xrow, crow, xn = (rows3[:, i * D:(i + 1) * D] for i in range(3))
        b2_all = rows3[:, :]
        gw_all = work[:, 0:D * NE]
        act = work[:, D * NE:D * NE + 2 * GT].rearrange("p (k t) -> p k t", k=2)
        rjunk = work[:, D * NE + 2 * GT:D * NE + 2 * GT + D]
        cst = sb("cst", [P, 4 * P])
        ident, m_text, m_vis, m_first = (cst[:, i * P:(i + 1) * P] for i in range(4))
        ssq = sb("ssq", [P, 3, GRP])
        ssk = sb("ssk", [P, 3, NB])
        half = sb("half", [P, GRP])
        nmax = sb("nmax", [P, GRP])
        rsum = sb("rsum", [P, GRP])
        rinv = sb("rinv", [P, GRP])
        small = sb("small", [P, 8])
        bnst = sb("bnst", [P, CELLS, 6])
        mom = sb("mom", [P, 5, CELLS])
        mean = sb("mean", [P, CELLS])
        vare = sb("vare", [P, CELLS])
        rstd = sb("rstd", [P, CELLS])
        tanh_x, tanh_f, kw = small[:, 2:3], small[:, 3:4], small[:, 6:7]

        w1_hi, w1_lo = kvt_hi[:, 0:FW], kvt_lo[:, 0:FW]
        w2_hi, w2_lo = w_hi[:, 0:FW], w_lo[:, 0:FW]
        hT_hi, hT_lo = (t[:, FW:FW + CH * GT].rearrange("p (c t) -> p c t", c=CH) for t in (kvt_hi, kvt_lo))
        a_hi, a_lo = (t[:, FW:FW + 2 * CH * GT].rearrange("p (k f t) -> p k f t", k=2, f=CH) for t in (w_hi, w_lo))
        h = raw[:, 0:CELLS, :]
        b1_sb = sb("b1_sb", [P, NE * CH])
        asum = sb("asum", [P, CELLS])
        hg = sb("hg", [P, CELLS, NE])
        gwl = sb("gwl", [P, NE])
        gb = sb("gb", [P, NE])
        rt = sb("rt", [P, 20, CELLS])
        r3 = sb("r3", [P, 8, CELLS, NE])
        pick = sb("pick", [P, 2, CELLS, NE])
        gate = sb("gate", [P, CELLS, NE])
        b2_sb = b2_all.rearrange("p (e d) -> p e d", e=NE)
        gw_sb = gw_all.rearrange("p (d e) -> p d e", e=NE)

        banks = [es.enter_context(nc.psum_tensor(f"bank{i}", [P, 512], fp32)) for i in range(8)]
        ps_q, ps_kv, ps_tq, ps_tk, ps_s, ps_tp, ps_o, ps_y = banks

        s_cst, s_par, s_tanh, s_prod, s_kw, s_init = (sem(n) for n in ("consts_in", "params_in", "tanh_ready", "wprod", "kw_ready", "zeroed"))
        ld = [sem(f"raw_in{i}") for i in range(RING)]
        w_hi_set, w_lo_set = sem("w_hi_set"), sem("w_lo_set")
        xrow_in, crow_in = sem("xrow_in"), sem("crow_in")
        st_a, st_b, st_c, ln_pow, xn_set = (sem(n) for n in ("ln_stats", "ln_moments", "ln_eps", "ln_rstd", "xn_set"))
        lat_t, ctx_t, lat_hi, lat_lo, ctx_hi, ctx_lo = (sem(n) for n in ("lat_transposed", "ctx_transposed", "lat_hi_set", "lat_lo_set", "ctx_hi_set", "ctx_lo_set"))
        y_next = sem("y_next")
        x2_out = sem("x2_out")
        q_done, kv_done, tqk_done, s_done, tp_done, o_done, y_done = (sem(n) for n in (
            "q_done", "kv_done", "qk_transposed", "scores_done", "p_transposed", "o_done", "y_done"))
        q_sq, q_sum, q_eps, q_pow, q_set = (sem(n) for n in ("q_squared", "q_summed", "q_eps", "q_rsqrt", "qhat_set"))
        k_sq, k_eps, k_pow, k_set = (sem(n) for n in ("k_squared", "k_eps", "k_rsqrt", "khat_set"))
        vhi_set, vlo_set, qT_set, kT_set = (sem(n) for n in ("v_hi_set", "v_lo_set", "qT_set", "kT_set"))
        max_set, exp_set, inv_set, p_set = (sem(n) for n in ("max_set", "exp_set", "inv_set", "p_set"))
        pThi_set, pTlo_set, oThi_set, oTlo_set, y_added = (sem(n) for n in ("pT_hi_set", "pT_lo_set", "oT_hi_set", "oT_lo_set", "y_added"))

        f_x2, f_stats, f_mom, f_eps, f_pow, f_h, f_abs, f_out = (sem(n) for n in (
            "f_x2_in", "f_stats", "f_moments", "f_eps", "f_rstd", "f_h_set", "f_abs_set", "f_out"))
        f_t, f_thi, f_tlo, f_w_hi, f_w_lo, f_bias = (sem(n) for n in (
            "f_transposed", "f_hT_hi", "f_hT_lo", "f_w_hi", "f_w_lo", "f_bias_in"))
        g1_done, g2_done, f_act, f_ahi, f_alo, f_yadd = (sem(n) for n in (
            "up_done", "down_done", "act_set", "act_hi_set", "act_lo_set", "expert_added"))
        r_sum, r_lgt, r_exp, r_top, r_pick, r_gate, r_hg, chain = (sem(n) for n in (
            "router_sums", "router_logits", "router_exp", "router_top", "router_picked", "gates_set", "router_dots", "dve_chain"))

        def wait(eng, s, value):
            if not isinstance(value, int) or value > 0:
                eng.wait_ge(s, value)

        def slot_count(b, j):
            first, second = (32 if k in (4, 5) else 16 for k in (j % RING, j % RING + RING))
            return b * (first + second) + (first if j < RING else first + second)

        def w_piece(t, par, j):
            return t[:, par * WCOLS + j * PIECE:par * WCOLS + (j + 1) * PIECE]

        def wq_at(t, par, c):
            return w_piece(t, par, c)

        def wkv_at(t, par, c):
            return t[:, par * WCOLS + 2048 + c * 256:par * WCOLS + 2048 + (c + 1) * 256]

        def wo_at(t, par, h):
            return w_piece(t, par, 6 + h)

        def kvt_cell(t, par, cell):
            if isinstance(cell, int):
                v = t[:, (par * CELLS + cell) * TILE:(par * CELLS + cell + 1) * TILE]
            else:
                v = t[:, bass.ds(par * CELLS * TILE + cell * TILE, TILE)]
            return v.rearrange("p (c n) -> p c n", c=CH)

        def prep_dst(t, par, cell, src):
            v = kvt_cell(t, par, cell)
            if src == 1:
                return v[:, :, S:3 * S]
            return v.rearrange("p c (r s) -> p c r s", r=4)[:, :, 0:4:3, :]

        def as_fp32(a):
            return a.bitcast(fp32)

        def bank_rows(b, src):
            v = b[:, :].rearrange("p (c t) -> p c t", c=CH)
            return v if src == 1 else v.rearrange("p c (b s) -> p c b s", b=NB)

        block = es.enter_context(nc.Block())

        @block.sync
        def _(sp):
            def load_piece(b, g, j):
                wait(sp, w_lo_set, b * PIECES + j - RING + 1 if not isinstance(b, int) or b * PIECES + j >= RING else 0)
                dst = raw[:, j % RING, :]
                if j < 4:
                    sp.dma_start(dst, wq_v[:, j, bass.ds(g * GRP * HD, PIECE)]).then_inc(ld[j % RING], 16)
                elif j < 6:
                    kv = dst.rearrange("p (c k n) -> p c k n", c=2, k=2)
                    c = 2 * (j - 4)
                    sp.dma_start(kv[:, :, 0, :], wk_v[:, c:c + 2, bass.ds(g * HD, HD)]).then_inc(ld[j % RING], 16)
                    sp.dma_start(kv[:, :, 1, :], wv_v[:, c:c + 2, bass.ds(g * HD, HD)]).then_inc(ld[j % RING], 16)
                else:
                    sp.dma_start(dst, wo_v[:, g * GRP + j - 6, :] if isinstance(g, int) else
                                 wo_v[:, bass.ds(g * GRP + j - 6, 1), :].rearrange("p a n -> p (a n)")).then_inc(ld[j % RING], 16)

            def load_rows(p, cell):
                wait(sp, xn_set, p)
                sp.dma_start(xrow[:, :], x_rows[:, bass.ds(cell, 1), :].rearrange("p a d -> p (a d)")).then_inc(xrow_in, 16)
                wait(sp, ctx_t, p)
                sp.dma_start(crow[:, :], c_rows[:, bass.ds(cell, 1), :].rearrange("p a d -> p (a d)")).then_inc(crow_in, 16)

            load_rows(0, 0)
            sp.dma_start(cst[:, :], consts).then_inc(s_cst, 16)
            for k, a in enumerate((g_xattn, g_ffn)):
                sp.dma_start(small[:, k:k + 1], a.partition_broadcast(P)).then_inc(s_par, 16)
            for k, a in enumerate((qnw, knw)):
                sp.dma_start(small[:, 4 + k:5 + k], a.rearrange("(p a) -> p a", a=1)).then_inc(s_par, 16)
            at = 0
            for p in range(CELLS):
                if p:
                    load_rows(p, p)
                for j in SPLITS[p]:
                    load_piece(0, 0, j)
                    at += 1
            for par in range(2):
                sp.dma_start(y[:, par * CELLS:(par + 1) * CELLS, :],
                             x_rows[:, par * CELLS:(par + 1) * CELLS, :]).then_inc(y_next, 16)
            load_rows(CELLS, CELLS)
            for j in range(PIECES):
                load_piece(1, 1, j)

            def iteration_loads(q, gp, last=False):
                it = q * ITS + gp
                wrap = isinstance(gp, int) and gp == ITS - 1
                for j in range(PIECES):
                    load_piece(it * 2 + 2, 0 if wrap else gp * 2 + 2, j)
                if last:
                    return
                for j in range(PIECES):
                    load_piece(it * 2 + 3, 1 if wrap else gp * 2 + 3, j)
                cell = it + CELLS + 1
                load_rows(cell, sp.snap(cell % (CELLS * QUARTERS)))

            iteration_loads(0, 0)
            with sp.Fori(0, QUARTERS - 1) as q:
                with sp.Fori(1, ITS - 1) as gp:
                    iteration_loads(q, gp)
                iteration_loads(q, ITS - 1)
                iteration_loads(q + 1, 0)
                done = y[:, bass.ds(sp.snap((q % 2) * CELLS), CELLS), :]
                coming = sp.snap((q + 2) % QUARTERS * CELLS)
                sp.wait_ge(y_added, (q + 1) * (STEPS * ITS) + 3)
                sp.dma_start(x2_rows[:, bass.ds(q * CELLS, CELLS), :], done).then_inc(x2_out, 16)
                sp.wait_ge(x2_out, (q + 1) * 16)
                sp.dma_start(done, x_rows[:, bass.ds(coming, CELLS), :]).then_inc(y_next, 16)
            with sp.Fori(1, ITS - 1) as gp:
                iteration_loads(QUARTERS - 1, gp)
            iteration_loads(QUARTERS - 1, ITS - 1, last=True)

            for k in range(2 * FPIECES):
                if k < RING:
                    sp.wait_ge(w_lo_set, (2 * NIT + 1) * PIECES + k - RING + 1)
                else:
                    sp.wait_ge(f_w_lo, k - RING + 1)
                v = w1_v if k < FPIECES else w2_v
                sp.dma_start(raw[:, k % RING, :], v[:, k % FPIECES, :]).then_inc(ld[k % RING], 16)
                if k == RING:
                    sp.wait_ge(ctx_t, NIT + CELLS)
                    sp.dma_start(b2_all, b2.rearrange("e d -> (e d)").partition_broadcast(P)).then_inc(f_bias, 16)
                    sp.dma_start(gwl[:, :], gate_w[D:D + 1, :].rearrange("d e -> (d e)").partition_broadcast(P)).then_inc(f_bias, 16)
                    sp.dma_start(gb[:, :], gate_b.partition_broadcast(P)).then_inc(f_bias, 16)
                    sp.dma_start(b1_sb[:, :], b1).then_inc(f_bias, 16)
            sp.wait_ge(y_added, NCELL + 3)
            sp.dma_start(gw_all, gate_w[0:D, :].rearrange("d e -> (d e)").partition_broadcast(P)).then_inc(f_bias, 16)
            par = (QUARTERS - 1) % 2
            sp.dma_start(x2_rows[:, (QUARTERS - 1) * CELLS:, :], y[:, par * CELLS:(par + 1) * CELLS, :]).then_inc(f_out, 16)
            sp.wait_ge(y_next, QUARTERS * 16 + 16)
            with sp.Fori(0, QUARTERS) as T:
                sp.wait_ge(f_out, T * 16 + 16)
                sp.dma_start(y[:, 0:CELLS, :], x2_rows[:, bass.ds(T * CELLS, CELLS), :]).then_inc(f_x2, 16)
                sp.wait_ge(f_yadd, T * NE * CELLS + NE * CELLS)
                sp.dma_start(o_rows[:, bass.ds(T * CELLS, CELLS), :], y[:, 0:CELLS, :]).then_inc(f_out, 16)
            sp.wait_ge(f_out, QUARTERS * 16 + 16)

        @block.gpsimd
        def _(pool):
            pow_ = lambda out, a, n: nc.gpsimd.tensor_tensor(out, a, half[:, 0:n], ALU.pow)

            def low_piece(b, j):
                pool.wait_ge(w_hi_set, b * PIECES + j + 1)
                par = low_piece.par
                nc.gpsimd.tensor_tensor(w_piece(w_lo, par, j), raw[:, j % RING, :], as_fp32(w_piece(w_hi, par, j)),
                                        ALU.subtract).then_inc(w_lo_set, 1)

            def ln_power(p):
                pool.wait_ge(st_c, p + 1)
                pow_(rstd[:, 0:1], vare[:, 0:1], 1).then_inc(ln_pow, 1)

            pool.wait_ge(s_init, 1)
            low_piece.par = 0
            for p in range(CELLS):
                ln_power(p)
                for j in SPLITS[p]:
                    low_piece(0, j)
            with pool.Fori(0, NIT) as it:
                for s in range(STEPS):
                    i = it * STEPS + s
                    pool.wait_ge(q_eps, i + 1)
                    pow_(ssq[:, 2, :], ssq[:, 1, :], GRP).then_inc(q_pow, 1)
                    low_piece.par = 1 - s // CELLS
                    for j in SPLITS[s % CELLS]:
                        low_piece(it * 2 + s // CELLS + 1, j)
                    pool.wait_ge(k_eps, i + 1)
                    pow_(ssk[:, 2, :], ssk[:, 1, :], NB).then_inc(k_pow, 1)
                    if s == 3:
                        ln_power(it + CELLS)
            with pool.Fori(0, QUARTERS) as T:
                pool.wait_ge(f_eps, T + 1)
                pow_(rstd[:, :], vare[:, :], CELLS).then_inc(f_pow, 1)

        @block.scalar
        def _(act_e):
            def high_piece(b, j, par):
                act_e.wait_ge(ld[j % RING], slot_count(b, j))
                nc.scalar.activation(w_piece(w_hi, par, j), raw[:, j % RING, :], ACT.Copy).then_inc(w_hi_set, 1)

            def q_part(i):
                act_e.wait_ge(q_done, i + 1)
                nc.scalar.activation(sq[:, :, :].rearrange("p g d -> p (g d)"), ps_q[:, :], ACT.Square).then_inc(q_sq, 1)

            def p_high(m):
                act_e.wait_ge(tp_done, m + 3)
                nc.scalar.activation(pT_hi[:, :, :].rearrange("p b r -> p (b r)"), ps_tp[:, :], ACT.Copy).then_inc(pThi_set, 1)

            def o_high(m):
                act_e.wait_ge(o_done, m + 3)
                nc.scalar.activation(oT_hi[:, :, :, :], ps_o[:, :].rearrange("p (b g s) -> p g b s", b=NB, g=GRP),
                                     ACT.Copy).then_inc(oThi_set, 1)

            def q_turned(m):
                act_e.wait_ge(tqk_done, m + 2)
                nc.scalar.activation(qT[:, :, :, :], ps_tq[:, :].rearrange("p (g b s) -> p b g s", g=GRP, b=NB),
                                     ACT.Copy).then_inc(qT_set, 1)

            def kv_part(i, s):
                act_e.wait_ge(kv_done, i + 1)
                kv = ps_kv[:, :].rearrange("p (b k d) -> p b k d", b=NB, k=2)
                for b in range(NB):
                    last = nc.scalar.activation(sqk[:, b, :], kv[:, b, 0, :], ACT.Square, accum_out=ssk[:, 0, b:b + 1])
                last.then_inc(k_sq, 1)
                nc.scalar.activation(v_hi[:, s % 2, :, :], kv[:, :, 1, :], ACT.Copy, scale=tanh_x).then_inc(vhi_set, 1)

            def softmax(m):
                act_e.wait_ge(max_set, m + 2)
                for r in range(GRP):
                    last = nc.scalar.activation(prob[:, r, :], ps_s[:, r * HD:(r + 1) * HD], ACT.Exp,
                                                bias=nmax[:, r:r + 1], accum_out=rsum[:, r:r + 1])
                last.then_inc(exp_set, 1)

            act_e.wait_ge(s_par, 64)
            nc.scalar.activation(small[:, 2:4], small[:, 0:2], ACT.Tanh).then_inc(s_tanh, 1)
            for p in range(CELLS):
                for j in SPLITS[p]:
                    high_piece(0, j, 0)
            act_e.wait_ge(s_tanh, 1)
            with act_e.Fori(0, NIT) as it:
                for s in range(STEPS):
                    i = it * STEPS + s
                    p_high(i - 2)
                    q_part(i)
                    if s % CELLS == 2:
                        act_e.wait_ge(y_done, i)
                    for j in SPLITS[s % CELLS]:
                        high_piece(it * 2 + s // CELLS + 1, j, 1 - s // CELLS)
                    o_high(i - 2)
                    q_turned(i - 1)
                    kv_part(i, s)
                    softmax(i - 1)
            p_high(NCELL - 2)
            o_high(NCELL - 2)
            q_turned(NCELL - 1)
            softmax(NCELL - 1)
            p_high(NCELL - 1)
            o_high(NCELL - 1)

            act_e.wait_ge(ctx_lo, NIT + CELLS)
            act_e.wait_ge(w_lo_set, (2 * NIT + 1) * PIECES)
            for k in range(2 * FPIECES):
                if k == FPIECES:
                    act_e.wait_ge(y_done, NCELL + 2)
                act_e.wait_ge(ld[k % RING], slot_count(2 * NIT, PIECES - RING + k % RING) + 16 * (k // RING + 1))
                dst = (w1_hi if k < FPIECES else w2_hi)[:, (k % FPIECES) * PIECE:(k % FPIECES + 1) * PIECE]
                nc.scalar.activation(dst, raw[:, k % RING, :], ACT.Copy).then_inc(f_w_hi, 1)
            act_e.wait_ge(f_bias, 80)
            with act_e.Fori(0, QUARTERS) as T:
                for c in range(CELLS):
                    act_e.wait_ge(f_h, T * CELLS + c + 1)
                    last = nc.scalar.activation(act[:, c % 2, :], h[:, c, :], ACT.Abs, accum_out=asum[:, c:c + 1])
                    if c % 2:
                        last.then_inc(f_abs, 1)
                        act_e.wait_ge(f_abs, T * 2 + c // 2 + 1)
                for c in range(CELLS):
                    act_e.wait_ge(f_t, T * CELLS + c + 1)
                    nc.scalar.activation(hT_hi[:, :, c * P:(c + 1) * P], banks[4 + c][:, :].rearrange("p (c t) -> p c t", c=CH),
                                         ACT.Copy).then_inc(f_thi, 1)
                for e, func in enumerate((ACT.Tanh, ACT.Gelu, ACT.Silu)):
                    for f in range(CH):
                        k = T * (NE * CH) + e * CH + f
                        act_e.wait_ge(g1_done, k + 1)
                        if e or f >= 2:
                            act_e.wait_ge(f_alo, k - 1)
                        nc.scalar.activation(act[:, f % 2, :], banks[f][:, :], func,
                                             bias=b1_sb[:, e * CH + f:e * CH + f + 1]).then_inc(f_act, 1)
                    if e == 0:
                        act_e.wait_ge(r_lgt, T + 1)
                        nc.scalar.activation(r3[:, 2, :, :], r3[:, 1, :, :], ACT.Exp).then_inc(r_exp, 1)

        @block.vector
        def _(dve):
            V = nc.vector

            def moments(n, summed, squared, done, count):
                stat = bnst[:, 0:n, :].rearrange("p c (k t) -> p c k t", k=2)
                dve.wait_ge(summed, count + 1)
                V.tensor_tensor(mom[:, 0, 0:n], stat[:, :, 0, 1], stat[:, :, 1, 1], ALU.add)
                V.tensor_tensor(mom[:, 1, 0:n], stat[:, :, 0, 1], stat[:, :, 1, 1], ALU.subtract)
                V.tensor_tensor(mom[:, 2, 0:n], stat[:, :, 0, 2], stat[:, :, 1, 2], ALU.add).then_inc(squared, 1)
                dve.wait_ge(squared, 2 * count + 1)
                V.tensor_scalar(mean[:, 0:n], mom[:, 0, 0:n], 0.5, None, ALU.mult)
                V.tensor_scalar(mom[:, 3, 0:n], mom[:, 2, 0:n], 1.0 / D, LN_EPS, ALU.mult, ALU.add)
                V.tensor_tensor(mom[:, 4, 0:n], mom[:, 1, 0:n], mom[:, 1, 0:n], ALU.mult).then_inc(squared, 1)
                dve.wait_ge(squared, 2 * count + 2)
                V.scalar_tensor_tensor(vare[:, 0:n], mom[:, 4, 0:n], 0.25, mom[:, 3, 0:n], ALU.mult, ALU.add).then_inc(done, 1)

            def ln_stats(p):
                dve.wait_ge(xrow_in, p * 16 + 16)
                V.bn_stats(bnst[:, 0, :], xrow).then_inc(st_a, 1)
                moments(1, st_a, st_b, st_c, p)

            def ln_apply(p):
                dve.wait_ge(ln_pow, p + 1)
                V.tensor_scalar(xn, xrow, mean[:, 0:1], rstd[:, 0:1], ALU.subtract, ALU.mult).then_inc(xn_set, 1)

            def rows_turned(p, par, cell, src):
                turned, hi_set, lo_set = ((ctx_t, ctx_hi, ctx_lo), (lat_t, lat_hi, lat_lo))[src]
                dst_hi, dst_lo = prep_dst(kvt_hi, par, cell, src), prep_dst(kvt_lo, par, cell, src)
                dve.wait_ge(turned, p + 1)
                V.tensor_scalar(dst_hi, bank_rows(ps_tq, src), 1.0, None, ALU.mult).then_inc(hi_set, 1)
                dve.wait_ge(hi_set, p + 1)
                V.tensor_tensor(dst_lo, bank_rows(ps_tq, src), as_fp32(dst_hi), ALU.subtract).then_inc(lo_set, 1)

            def scale_q(i, s):
                dve.wait_ge(q_pow, i + 1)
                V.tensor_tensor(qhat[:, s % 2, :, :], ps_q[:, :].rearrange("p (g d) -> p g d", g=GRP),
                                ssq[:, 2, :].unsqueeze(2).to_broadcast([P, GRP, HD]), ALU.mult).then_inc(q_set, 1)

            def sum_q(i):
                dve.wait_ge(q_sq, i + 1)
                V.tensor_reduce(ssq[:, 0, :], sq[:, :, :], AX.X, ALU.add).then_inc(q_sum, 1)
                dve.wait_ge(q_sum, i + 1)
                V.tensor_scalar(ssq[:, 1, :], ssq[:, 0, :], RMS_EPS * HD, None, ALU.add).then_inc(q_eps, 1)

            def p_low(m):
                dve.wait_ge(pThi_set, m + 3)
                V.tensor_tensor(pT_lo[:, :, :].rearrange("p b r -> p (b r)"), ps_tp[:, :],
                                as_fp32(pT_hi[:, :, :]).rearrange("p b r -> p (b r)"), ALU.subtract).then_inc(pTlo_set, 1)

            def o_low(m):
                dve.wait_ge(oThi_set, m + 3)
                V.tensor_tensor(oT_lo[:, :, :, :], ps_o[:, :].rearrange("p (b g s) -> p g b s", b=NB, g=GRP),
                                as_fp32(oT_hi[:, :, :, :]), ALU.subtract).then_inc(oTlo_set, 1)

            def k_turned(m):
                dve.wait_ge(tqk_done, m + 2)
                V.tensor_scalar(kT[:, :, :].rearrange("p b k -> p (b k)"), ps_tk[:, 0:NB * HD], kw, None, ALU.mult).then_inc(kT_set, 1)

            def k_sum_v_low(i, s):
                dve.wait_ge(k_sq, i + 1)
                V.tensor_scalar(ssk[:, 1, :], ssk[:, 0, :], RMS_EPS * HD, None, ALU.add).then_inc(k_eps, 1)
                kv = ps_kv[:, :].rearrange("p (b k d) -> p b k d", b=NB, k=2)
                dve.wait_ge(vhi_set, i + 1)
                V.scalar_tensor_tensor(v_lo[:, s % 2, :, :], kv[:, :, 1, :], tanh_x, as_fp32(v_hi[:, s % 2, :, :]),
                                       ALU.mult, ALU.subtract).then_inc(vlo_set, 1)

            def row_max(m):
                dve.wait_ge(s_done, m + 2)
                V.tensor_reduce(nmax[:, :], ps_s[:, :].rearrange("p (r k) -> p r k", r=GRP), AX.X, ALU.max,
                                negate=True).then_inc(max_set, 1)

            def scale_k(i):
                dve.wait_ge(k_pow, i + 1)
                kv = ps_kv[:, :].rearrange("p (b k d) -> p b k d", b=NB, k=2)
                V.tensor_tensor(khat[:, :, :], kv[:, :, 0, :], ssk[:, 2, :].unsqueeze(2).to_broadcast([P, NB, HD]),
                                ALU.mult).then_inc(k_set, 1)

            def normalise(m):
                dve.wait_ge(exp_set, m + 2)
                V.reciprocal(rinv[:, :], rsum[:, :]).then_inc(inv_set, 1)
                dve.wait_ge(inv_set, m + 2)
                V.tensor_tensor(prob[:, :, :], prob[:, :, :], rinv[:, :].unsqueeze(2).to_broadcast([P, GRP, HD]),
                                ALU.mult).then_inc(p_set, 1)

            def add_y(m, c):
                dve.wait_ge(y_done, m + 3)
                slot = (m + 2 * STEPS * ITS) // (STEPS * ITS) % 2 * CELLS + c
                yt = y[:, slot, :] if isinstance(slot, int) else y[:, bass.ds(slot, 1), :].rearrange("p a d -> p (a d)")
                V.tensor_tensor(yt, ps_y[:, :], yt, ALU.add).then_inc(y_added, 1)

            V.memset(as_fp32(v_hi[:, :, :, :]).rearrange("p k b d -> p (k b d)"), 0.0)
            V.memset(as_fp32(v_lo[:, :, :, :]).rearrange("p k b d -> p (k b d)"), 0.0).then_inc(vlo_set, 1)
            V.memset(as_fp32(w_hi[:, WCOLS + 6 * PIECE:2 * WCOLS]), 0.0)
            V.memset(as_fp32(w_lo[:, WCOLS + 6 * PIECE:2 * WCOLS]), 0.0).then_inc(y_added, 1)
            V.memset(qhat[:, 1, :, :].rearrange("p g d -> p (g d)"), 0.0).then_inc(q_set, 1)
            V.memset(khat[:, :, :].rearrange("p b d -> p (b d)"), 0.0).then_inc(k_set, 1)
            V.memset(prob[:, :, :].rearrange("p g d -> p (g d)"), 0.0).then_inc(p_set, 1)
            V.memset(half[:, :], -0.5).then_inc(s_init, 1)
            dve.wait_ge(s_par, 64)
            V.tensor_tensor(small[:, 7:8], small[:, 4:5], small[:, 5:6], ALU.mult).then_inc(s_prod, 1)
            dve.wait_ge(s_prod, 1)
            V.tensor_scalar(kw, small[:, 7:8], float(HD) ** 0.5, None, ALU.mult).then_inc(s_kw, 1)
            dve.wait_ge(s_kw, 1)
            dve.wait_ge(s_tanh, 1)
            for p in range(CELLS):
                ln_stats(p)
                ln_apply(p)
                rows_turned(p, 0, p, 1)
                rows_turned(p, 0, p, 0)
            dve.wait_ge(y_next, 32)
            with dve.Fori(0, NIT) as it:
                for s in range(STEPS):
                    i = it * STEPS + s
                    p = it + CELLS
                    p_low(i - 2)
                    sum_q(i)
                    scale_q(i, s)
                    k_turned(i - 1)
                    o_low(i - 2)
                    k_sum_v_low(i, s)
                    row_max(i - 1)
                    scale_k(i)
                    normalise(i - 1)
                    if s in (5, 6):
                        rows_turned(p, 0, (it // ITS + 1) % 2 * CELLS + it % ITS, 6 - s)
                    if s == 0:
                        dve.wait_ge(y_next, it // ITS * 16 + 16)
                    add_y(i - 2, (s - 2) % CELLS)
                    if s == 3:
                        ln_stats(p)
                    if s == 4:
                        ln_apply(p)
            p_low(NCELL - 2)
            o_low(NCELL - 2)
            k_turned(NCELL - 1)
            row_max(NCELL - 1)
            normalise(NCELL - 1)
            add_y(NCELL - 2, CELLS - 2)
            p_low(NCELL - 1)
            o_low(NCELL - 1)
            add_y(NCELL - 1, CELLS - 1)

            for k in range(2 * FPIECES):
                dve.wait_ge(f_w_hi, k + 1)
                hi, lo = (w1_hi, w1_lo) if k < FPIECES else (w2_hi, w2_lo)
                a, z = (k % FPIECES) * PIECE, (k % FPIECES + 1) * PIECE
                V.tensor_tensor(lo[:, a:z], raw[:, k % RING, :], as_fp32(hi[:, a:z]), ALU.subtract).then_inc(f_w_lo, 1)
            dve.wait_ge(f_bias, 80)
            dve.wait_ge(f_w_lo, 2 * FPIECES)

            with dve.Fori(0, QUARTERS) as T:
                links = [0]

                def link(ins):
                    links[0] += 1
                    ins.then_inc(chain, 1)
                    dve.wait_ge(chain, T * CHAIN + links[0])

                dve.wait_ge(f_x2, T * 16 + 16)
                for c in range(CELLS):
                    last = V.bn_stats(bnst[:, c, :], y[:, c, :])
                last.then_inc(f_stats, 1)
                moments(CELLS, f_stats, f_mom, f_eps, T)
                dve.wait_ge(f_pow, T + 1)
                for c in range(CELLS):
                    V.tensor_scalar(h[:, c, :], y[:, c, :], mean[:, c:c + 1], rstd[:, c:c + 1], ALU.subtract, ALU.mult).then_inc(f_h, 1)
                for c in range(CELLS):
                    dve.wait_ge(f_thi, T * CELLS + c + 1)
                    V.tensor_tensor(hT_lo[:, :, c * P:(c + 1) * P], banks[4 + c][:, :].rearrange("p (c t) -> p c t", c=CH),
                                    as_fp32(hT_hi[:, :, c * P:(c + 1) * P]), ALU.subtract).then_inc(f_tlo, 1)

                def split_act(e, f):
                    k = T * (NE * CH) + e * CH + f
                    dve.wait_ge(f_act, k + 1)
                    V.tensor_copy(a_hi[:, e % 2, f, :], act[:, f % 2, :]).then_inc(f_ahi, 1)
                    dve.wait_ge(f_ahi, k + 1)
                    V.tensor_tensor(a_lo[:, e % 2, f, :], act[:, f % 2, :], as_fp32(a_hi[:, e % 2, f, :]),
                                    ALU.subtract).then_inc(f_alo, 1)

                def add_expert(e, c):
                    n = T * (NE * CELLS) + e * CELLS + c
                    dve.wait_ge(g2_done, n + 1)
                    V.scalar_tensor_tensor(y[:, c, :], banks[4 + c][:, :], gate[:, c, e:e + 1], y[:, c, :],
                                           ALU.mult, ALU.add).then_inc(f_yadd, 1)

                for f in range(CH):
                    split_act(0, f)

                for c in range(CELLS):
                    for e in range(NE):
                        last = V.tensor_tensor_reduce(out=rjunk, in0=h[:, c, :], in1=gw_sb[:, :, e], scale=1.0, scalar=0.0,
                                                      op0=ALU.mult, op1=ALU.add, accum_out=hg[:, c, e:e + 1])
                        link(last)
                bc = lambda a: a.unsqueeze(2).to_broadcast([P, CELLS, NE])
                be = lambda a: a.unsqueeze(1).to_broadcast([P, CELLS, NE])
                dve.wait_ge(r_sum, T + 1)
                V.tensor_scalar(rt[:, 0, :], banks[4][:, 0:CELLS], 1.0 / ((S - VIS) * D), None, ALU.mult)
                link(V.tensor_scalar(rt[:, 1, :], banks[4][:, CELLS:2 * CELLS], 1.0 / (VIS * D), 1e-8, ALU.mult, ALU.add))
                link(V.reciprocal(rt[:, 2, :], rt[:, 1, :]))
                link(V.tensor_tensor(rt[:, 3, :], rt[:, 0, :], rt[:, 2, :], ALU.mult))
                link(V.tensor_tensor(r3[:, 0, :, :], bc(rt[:, 3, :]), be(gwl[:, :]), ALU.mult))
                link(V.tensor_tensor(r3[:, 3, :, :], r3[:, 0, :, :], hg[:, :, :], ALU.add))
                link(V.tensor_tensor(r3[:, 4, :, :], r3[:, 3, :, :], be(gb[:, :]), ALU.add))
                link(V.tensor_reduce(rt[:, 4, :], r3[:, 4, :, :], AX.X, ALU.max))
                V.tensor_tensor(r3[:, 1, :, :], r3[:, 4, :, :], bc(rt[:, 4, :]), ALU.subtract).then_inc(r_lgt, 1)
                dve.wait_ge(r_exp, T + 1)
                link(V.tensor_reduce(rt[:, 5, :], r3[:, 2, :, :], AX.X, ALU.add))
                link(V.reciprocal(rt[:, 6, :], rt[:, 5, :]))
                score = r3[:, 5, :, :]
                link(V.tensor_tensor(score, r3[:, 2, :, :], bc(rt[:, 6, :]), ALU.mult))
                s0, s1, s2 = (r3[:, 5, :, e] for e in range(NE))
                c01, c02, c12 = rt[:, 7, :], rt[:, 8, :], rt[:, 9, :]
                V.tensor_tensor(c01, s0, s1, ALU.is_ge)
                V.tensor_tensor(c02, s0, s2, ALU.is_ge)
                link(V.tensor_tensor(c12, s1, s2, ALU.is_ge))
                rank = r3[:, 6, :, :]
                V.tensor_tensor(rt[:, 10, :], c01, c02, ALU.add)
                V.tensor_tensor(rt[:, 11, :], c01, c12, ALU.subtract)
                link(V.tensor_tensor(r3[:, 6, :, 2], c02, c12, ALU.add))
                V.tensor_scalar(r3[:, 6, :, 0], rt[:, 10, :], -1.0, 2.0, ALU.mult, ALU.add)
                link(V.tensor_scalar(r3[:, 6, :, 1], rt[:, 11, :], 1.0, None, ALU.add))
                V.tensor_scalar(pick[:, 0, :, :], rank, 0.0, None, ALU.is_equal)
                V.tensor_scalar(pick[:, 1, :, :], rank, 1.0, None, ALU.is_equal).then_inc(r_top, 1)
                dve.wait_ge(r_top, T + 1)
                V.tensor_reduce(rt[:, 12, :], score, AX.X, ALU.max)
                link(V.tensor_tensor(r3[:, 7, :, :], score, pick[:, 1, :, :], ALU.mult))
                link(V.tensor_reduce(rt[:, 13, :], r3[:, 7, :, :], AX.X, ALU.add))
                link(V.scalar_tensor_tensor(rt[:, 14, :], rt[:, 12, :], 1e-8, rt[:, 13, :], ALU.add, ALU.add))
                link(V.reciprocal(rt[:, 15, :], rt[:, 14, :]))
                link(V.tensor_scalar(rt[:, 16, :], rt[:, 15, :], tanh_f, None, ALU.mult))
                V.tensor_tensor(rt[:, 17, :], rt[:, 12, :], rt[:, 16, :], ALU.mult)
                link(V.tensor_tensor(rt[:, 18, :], rt[:, 13, :], rt[:, 16, :], ALU.mult))

                for f in range(CH):
                    split_act(1, f)
                dve.wait_ge(r_pick, T + 1)
                picked = banks[4][:, 0:2 * CELLS * NE].rearrange("p (k c e) -> p k c e", k=2, c=CELLS)
                V.tensor_tensor(r3[:, 0, :, :], picked[:, 0, :, :], bc(rt[:, 17, :]), ALU.mult)
                link(V.tensor_tensor(r3[:, 3, :, :], picked[:, 1, :, :], bc(rt[:, 18, :]), ALU.mult))
                V.tensor_tensor(gate[:, :, :], r3[:, 0, :, :], r3[:, 3, :, :], ALU.add).then_inc(r_gate, 1)
                dve.wait_ge(r_gate, T + 1)
                for e in range(NE):
                    for c in range(CELLS):
                        last = V.scalar_tensor_tensor(y[:, c, :], b2_sb[:, e, :], gate[:, c, e:e + 1], y[:, c, :], ALU.mult, ALU.add)
                    link(last)
                for c in range(CELLS):
                    add_expert(0, c)
                for f in range(CH):
                    split_act(2, f)
                for e in (1, 2):
                    for c in range(CELLS):
                        dve.wait_ge(f_yadd, T * (NE * CELLS) + (e - 1) * CELLS + c + 1)
                        add_expert(e, c)
                assert links[0] == CHAIN, links

        @block.tensor
        def _(pe):
            mm = nc.tensor.matmul

            def split_product(out, pairs, before_last=None):
                n = len(pairs)
                for k, (a_hi_, a_lo_, b_hi_, b_lo_) in enumerate(pairs):
                    if before_last is not None and k == n - 1:
                        before_last()
                    mm(out, a_hi_, b_hi_, start=k == 0, stop=False)
                    mm(out, a_hi_, b_lo_, start=False, stop=False)
                    last = mm(out, a_lo_, b_hi_, start=False, stop=k == n - 1)
                return last

            def turn(p, src):
                if src == 1:
                    pe.wait_ge(xn_set, p + 1)
                    rows, done = xn, lat_t
                else:
                    pe.wait_ge(crow_in, p * 16 + 16)
                    rows, done = crow, ctx_t
                for c in range(CH):
                    last = nc.tensor.transpose(ps_tq[:, c * P:(c + 1) * P], rows[:, c * P:(c + 1) * P], ident)
                last.then_inc(done, 1)

            def project_q(m, kpar, cell, wpar):
                hi, lo = kvt_cell(kvt_hi, kpar, cell), kvt_cell(kvt_lo, kpar, cell)
                return split_product(ps_q[:, :], [(hi[:, c, S:3 * S], lo[:, c, S:3 * S], wq_at(w_hi, wpar, c), wq_at(w_lo, wpar, c))
                                                  for c in range(CH)], before_last=lambda: turn_p(m))

            def project_kv(b, kpar, cell, wpar):
                hi, lo = kvt_cell(kvt_hi, kpar, cell), kvt_cell(kvt_lo, kpar, cell)
                rows = lambda t, c: t[:, c, b * 2 * S:(b + 1) * 2 * S]
                return split_product(ps_kv[:, b * 2 * HD:(b + 1) * 2 * HD], [
                    (rows(hi, c), rows(lo, c), wkv_at(w_hi, wpar, c), wkv_at(w_lo, wpar, c)) for c in range(CH)])

            def turn_p(m):
                pe.wait_ge(p_set, m + 3)
                for r in range(GRP):
                    last = nc.tensor.transpose(ps_tp[:, r * P:(r + 1) * P], prob[:, r, :], ident)
                last.then_inc(tp_done, 1)

            def weigh_v(m, s):
                pe.wait_ge(pTlo_set, m + 3)
                for b in range(NB):
                    k = s % 2
                    last = split_product(ps_o[:, b * GRP * S:(b + 1) * GRP * S], [
                        (v_hi[:, k, b, :], v_lo[:, k, b, :], pT_hi[:, b, :], pT_lo[:, b, :])])
                last.then_inc(o_done, 1)

            def turn_qk(m, s):
                for g in range(GRP):
                    nc.tensor.transpose(ps_tq[:, g * P:(g + 1) * P], qhat[:, s % 2, g, :], ident)
                for b in range(NB):
                    last = nc.tensor.transpose(ps_tk[:, b * P:(b + 1) * P], khat[:, b, :], ident)
                last.then_inc(tqk_done, 1)

            def scores(m):
                pe.wait_ge(qT_set, m + 2)
                pe.wait_ge(kT_set, m + 2)
                for r in range(GRP):
                    b, g = r // 2, r % 2 * 2
                    last = mm(ps_s[:, r * HD:(r + 1) * HD], qT[:, b, g:g + 2, :].rearrange("p g s -> p (g s)"), kT[:, b, :],
                              start=True, stop=True)
                last.then_inc(s_done, 1)

            def project_o(m, wpar):
                pe.wait_ge(oTlo_set, m + 3)
                flat = lambda t, h: t[:, h, :, :].rearrange("p b s -> p (b s)")
                split_product(ps_y[:, :], [(flat(oT_hi, h), flat(oT_lo, h), wo_at(w_hi, wpar, h), wo_at(w_lo, wpar, h))
                                           for h in range(GRP)]).then_inc(y_done, 1)

            pe.wait_ge(s_cst, 16)
            for p in range(CELLS):
                if p:
                    pe.wait_ge(ctx_lo, p)
                turn(p, 1)
                pe.wait_ge(lat_lo, p + 1)
                turn(p, 0)
            with pe.Fori(0, QUARTERS // 2) as j:
                for kpar in range(2):
                    with pe.Fori(0, ITS) as gp:
                        it = (j * 2 + kpar) * ITS + gp
                        pe.wait_ge(ctx_lo, (j * 2 + kpar) * CELLS + CELLS)
                        for s in range(STEPS):
                            i, blk, cell, wpar = it * STEPS + s, it * 2 + s // CELLS, s % CELLS, s // CELLS
                            if cell == 0:
                                pe.wait_ge(w_lo_set, blk * PIECES + 4)
                            pe.wait_ge(q_set, i + 1)
                            project_q(i - 2, kpar, cell, wpar).then_inc(q_done, 1)
                            if cell == 0:
                                pe.wait_ge(w_lo_set, blk * PIECES + 6)
                            pe.wait_ge(vlo_set, i + 1)
                            pe.wait_ge(k_set, i + 1)
                            project_kv(0, kpar, cell, wpar)
                            weigh_v(i - 2, s)
                            if s == 0:
                                pe.wait_ge(ctx_lo, it + CELLS)
                            if s == 6:
                                pe.wait_ge(lat_lo, it + CELLS + 1)
                            if s == 7:
                                pe.wait_ge(ctx_lo, it + CELLS + 1)
                            turn_qk(i - 1, s - 1)
                            project_kv(1, kpar, cell, wpar).then_inc(kv_done, 1)
                            scores(i - 1)
                            if s in (5, 6):
                                turn(it + CELLS, 6 - s)
                            if cell == 2:
                                pe.wait_ge(w_lo_set, blk * PIECES + PIECES)
                            pe.wait_ge(y_added, i + 1)
                            project_o(i - 2, wpar if cell >= 2 else 1 - wpar)
            pe.wait_ge(q_set, NCELL + 1)
            pe.wait_ge(k_set, NCELL + 1)
            turn_p(NCELL - 2)
            weigh_v(NCELL - 2, 0)
            turn_qk(NCELL - 1, 1)
            scores(NCELL - 1)
            pe.wait_ge(y_added, NCELL + 1)
            project_o(NCELL - 2, 1)
            turn_p(NCELL - 1)
            weigh_v(NCELL - 1, 1)
            pe.wait_ge(y_added, NCELL + 2)
            project_o(NCELL - 1, 1)

            pe.wait_ge(f_w_lo, 2 * FPIECES)
            pe.wait_ge(y_added, NCELL + 3)
            with pe.Fori(0, QUARTERS) as T:
                def up(e):
                    for f in range(CH):
                        k = T * (NE * CH) + e * CH + f
                        if e:
                            pe.wait_ge(f_act, k - CH + 1)
                        at = lambda t, c: t[:, (e * CH + c) * D + f * P:(e * CH + c) * D + (f + 1) * P]
                        split_product(banks[f][:, :], [(at(w1_hi, c), at(w1_lo, c), hT_hi[:, c, :], hT_lo[:, c, :])
                                                       for c in range(CH)]).then_inc(g1_done, 1)

                def down(e):
                    pe.wait_ge(f_alo, T * (NE * CH) + (e + 1) * CH)
                    for c in range(CELLS):
                        if e:
                            pe.wait_ge(f_yadd, T * (NE * CELLS) + (e - 1) * CELLS + c + 1)
                        at = lambda t, f: t[:, (e * CH + f) * D:(e * CH + f + 1) * D]
                        split_product(banks[4 + c][:, :], [
                            (a_hi[:, e % 2, f, c * P:(c + 1) * P], a_lo[:, e % 2, f, c * P:(c + 1) * P], at(w2_hi, f), at(w2_lo, f))
                            for f in range(CH)]).then_inc(g2_done, 1)

                for c in range(CELLS):
                    pe.wait_ge(f_h, T * CELLS + c + 1)
                    for k in range(CH):
                        last = nc.tensor.transpose(banks[4 + c][:, k * P:(k + 1) * P], h[:, c, k * P:(k + 1) * P], ident)
                    last.then_inc(f_t, 1)
                pe.wait_ge(f_tlo, T * CELLS + CELLS)
                up(0)
                pe.wait_ge(f_abs, T * 2 + 2)
                mm(banks[4][:, 0:CELLS], m_text, asum[:, :], start=True, stop=True)
                mm(banks[4][:, CELLS:2 * CELLS], m_vis, asum[:, :], start=True, stop=True).then_inc(r_sum, 1)
                up(1)
                pe.wait_ge(r_top, T + 1)
                mm(banks[4][:, 0:2 * CELLS * NE], m_first, pick[:, :, :, :].rearrange("p k c e -> p (k c e)"),
                   start=True, stop=True).then_inc(r_pick, 1)
                pe.wait_ge(r_gate, T + 1)
                down(0)
                up(2)
                down(1)
                down(2)


_INS = ["x", "ctx_4096", "g_xattn", "g_ffn", "L0_xattn_Wq", "L0_xattn_Wk", "L0_xattn_Wv", "L0_xattn_Wo",
        "L0_xattn_q_norm_w", "L0_xattn_k_norm_w", "L0_ffn_gate_w", "L0_ffn_gate_b", "L0_ffn_w1", "L0_ffn_b1",
        "L0_ffn_w2", "L0_ffn_b2"]


def kernel(**inputs):
    import numpy as np
    import concourse.bacc as bacc
    from concourse.bass_utils import run_bass_kernel_spmd

    n = np.arange(P)
    same = n[:, None] // S == n[None, :] // S
    late = (n[:, None] % S >= VIS)
    consts = np.concatenate([np.eye(P), same & late, same & ~late, same & (n[:, None] % S == 0)], axis=1).astype(np.float32)

    nc = bacc.Bacc("TRN2", target_bir_lowering=False, num_devices=1)
    arrays, args = {}, []
    for name in _INS:
        a = np.ascontiguousarray(inputs[name])
        if name == "L0_ffn_b1":
            a = np.ascontiguousarray(a.reshape(NE * CH, P).T)
        arrays[f"in_{name}"] = a
        args.append(nc.dram_tensor(f"in_{name}", a.shape, mybir.dt.from_np(a.dtype), kind="ExternalInput").ap())
    arrays["consts"] = consts
    args.append(nc.dram_tensor("consts", consts.shape, mybir.dt.float32, kind="ExternalInput").ap())
    args.append(nc.dram_tensor("x2_scratch", (B * S, D), mybir.dt.float32, kind="Internal").ap())
    args.append(nc.dram_tensor("out", (B, S, D), mybir.dt.float32, kind="ExternalOutput").ap())
    flamingo_block(nc, *args)
    r = run_bass_kernel_spmd(nc, [arrays], core_ids=[0])
    return r.results[0]["out"]
```

```python
import concourse.bass as bass
from concourse import mybir
from contextlib import ExitStack

B, S, D = 32, 64, 512
HEADS, KVH, HD = 32, 8, 128
GRP = HEADS // KVH
NE = 3
P = 128
CH = D // P
NB = P // S
CELLS = 4
QUARTERS = B // (NB * CELLS)
ITS = KVH // 2
NIT = QUARTERS * ITS
STEPS = 2 * CELLS
NCELL = NIT * STEPS
PIECE = 512
PIECES = 10
RING = 5
WCOLS = PIECES * PIECE
SPLITS = [(0, 1, 2), (3, 4, 5), (6, 7), (8, 9)]
TILE = CH * NB * 2 * S
VIS = int(S * 0.3)
LN_EPS, RMS_EPS = 1e-5, 1e-6
FW = NE * CH * D
FPIECES = FW // PIECE
FEARLY = PIECES
FLATE = 2 * FPIECES - FEARLY
GT = P * CELLS
CHAIN = 23


def flamingo_block(nc, x, ctx_rows, g_xattn, g_ffn, wq, wk, wv, wo, qnw, knw, gate_w, gate_b, w1, b1, w2, b2, consts, x2_dram, out):
    fp32, f32r = mybir.dt.float32, mybir.dt.float32r
    ALU, ACT, AX = mybir.AluOpType, mybir.ActivationFunctionType, mybir.AxisListType

    x_rows = x.rearrange("b s d -> (b s) d").rearrange("(c p) d -> p c d", p=P)
    c_rows = ctx_rows.rearrange("b s d -> (b s) d").rearrange("(c p) d -> p c d", p=P)
    x2_rows = x2_dram.rearrange("(c p) d -> p c d", p=P)
    o_rows = out.rearrange("b s d -> (b s) d").rearrange("(c p) d -> p c d", p=P)
    wq_v = wq.rearrange("(c p) n -> p c n", p=P)
    wk_v = wk.rearrange("(c p) n -> p c n", p=P)
    wv_v = wv.rearrange("(c p) n -> p c n", p=P)
    wo_v = wo.rearrange("(h p) n -> p h n", p=P)
    w1_v = w1.rearrange("e (c p) n -> p (e c) n", p=P)
    w2_v = w2.rearrange("e (c p) n -> p (e c) n", p=P)

    es = ExitStack()
    with es:
        def sb(name, shape, dt=fp32):
            return es.enter_context(nc.sbuf_tensor(name, shape, dt))

        def sem(name):
            return es.enter_context(nc.semaphore(name))

        kvt_hi = sb("kvt_hi", [P, 2 * CELLS * TILE], f32r)
        kvt_lo = sb("kvt_lo", [P, 2 * CELLS * TILE], f32r)
        w_hi = sb("w_hi", [P, 2 * WCOLS], f32r)
        w_lo = sb("w_lo", [P, 2 * WCOLS], f32r)
        raw = sb("raw", [P, RING, PIECE])
        y = sb("y", [P, 2 * CELLS, D])
        work = sb("work", [P, 26 * HD])
        at = [0]

        def part(k):
            at[0] += k * HD
            return work[:, at[0] - k * HD:at[0]]

        qhat = part(2 * GRP).rearrange("p (k g d) -> p k g d", k=2, g=GRP)
        khat = part(NB).rearrange("p (b d) -> p b d", b=NB)
        qT = part(GRP).rearrange("p (b g s) -> p b g s", b=NB, g=GRP)
        kT = part(NB).rearrange("p (b k) -> p b k", b=NB)
        prob = part(GRP).rearrange("p (r k) -> p r k", r=GRP)
        sq = part(GRP).rearrange("p (g d) -> p g d", g=GRP)
        sqk = part(NB).rearrange("p (b d) -> p b d", b=NB)
        parts = sb("parts", [P, 6 * PIECE], f32r)
        v_hi, v_lo = (parts[:, i * PIECE:(i + 1) * PIECE].rearrange("p (k b d) -> p k b d", k=2, b=NB) for i in (0, 1))
        pT_hi, pT_lo = (parts[:, i * PIECE:(i + 1) * PIECE].rearrange("p (b r) -> p b r", b=NB) for i in (2, 3))
        oT_hi, oT_lo = (parts[:, i * PIECE:(i + 1) * PIECE].rearrange("p (g b s) -> p g b s", g=GRP, b=NB) for i in (4, 5))
        rows3 = sb("rows3", [P, 3 * D])
        xrow, crow, xn = (rows3[:, i * D:(i + 1) * D] for i in range(3))
        gw_all = rows3[:, :]
        b2_all = work[:, 0:D * NE]
        act = work[:, D * NE:D * NE + 2 * GT].rearrange("p (k t) -> p k t", k=2)
        rjunk = work[:, D * NE + 2 * GT:D * NE + 2 * GT + D]
        cst = sb("cst", [P, 4 * P])
        ident, m_text, m_vis, m_first = (cst[:, i * P:(i + 1) * P] for i in range(4))
        ssq = sb("ssq", [P, 3, GRP])
        ssk = sb("ssk", [P, 3, NB])
        half = sb("half", [P, GRP])
        nmax = sb("nmax", [P, GRP])
        rsum = sb("rsum", [P, GRP])
        rinv = sb("rinv", [P, GRP])
        small = sb("small", [P, 8])
        bnst = sb("bnst", [P, CELLS, 6])
        mom = sb("mom", [P, 5, CELLS])
        mean = sb("mean", [P, CELLS])
        vare = sb("vare", [P, CELLS])
        rstd = sb("rstd", [P, CELLS])
        tanh_x, tanh_f, kw = small[:, 2:3], small[:, 3:4], small[:, 6:7]

        w1_hi, w1_lo = kvt_hi[:, 0:FW], kvt_lo[:, 0:FW]
        w2_hi, w2_lo = w_hi[:, 0:FW], w_lo[:, 0:FW]
        hT_hi, hT_lo = (t[:, FW:FW + CH * GT].rearrange("p (c t) -> p c t", c=CH) for t in (kvt_hi, kvt_lo))
        a_hi, a_lo = (t[:, FW:FW + 2 * CH * GT].rearrange("p (k f t) -> p k f t", k=2, f=CH) for t in (w_hi, w_lo))
        h = raw[:, 0:CELLS, :]
        b1_sb = sb("b1_sb", [P, NE * CH])
        asum = sb("asum", [P, CELLS])
        hg = sb("hg", [P, CELLS, NE])
        gwl = sb("gwl", [P, NE])
        gb = sb("gb", [P, NE])
        rt = sb("rt", [P, 20, CELLS])
        r3 = sb("r3", [P, 8, CELLS, NE])
        pick = sb("pick", [P, 2, CELLS, NE])
        gate = sb("gate", [P, CELLS, NE])
        b2_sb = b2_all.rearrange("p (e d) -> p e d", e=NE)
        gw_sb = gw_all.rearrange("p (d e) -> p d e", e=NE)

        banks = [es.enter_context(nc.psum_tensor(f"bank{i}", [P, 512], fp32)) for i in range(8)]
        ps_q, ps_kv, ps_tq, ps_tk, ps_s, ps_tp, ps_o, ps_y = banks

        s_cst, s_par, s_tanh, s_prod, s_kw, s_init = (sem(n) for n in ("consts_in", "params_in", "tanh_ready", "wprod", "kw_ready", "zeroed"))
        ld = [sem(f"raw_in{i}") for i in range(RING)]
        w_hi_set, w_lo_set = sem("w_hi_set"), sem("w_lo_set")
        xrow_in, crow_in = sem("xrow_in"), sem("crow_in")
        st_a, st_b, st_c, ln_pow, xn_set = (sem(n) for n in ("ln_stats", "ln_moments", "ln_eps", "ln_rstd", "xn_set"))
        lat_t, ctx_t, lat_hi, lat_lo, ctx_hi, ctx_lo = (sem(n) for n in ("lat_transposed", "ctx_transposed", "lat_hi_set", "lat_lo_set", "ctx_hi_set", "ctx_lo_set"))
        y_next = sem("y_next")
        x2_out = sem("x2_out")
        q_done, kv_done, tqk_done, s_done, tp_done, o_done, y_done = (sem(n) for n in (
            "q_done", "kv_done", "qk_transposed", "scores_done", "p_transposed", "o_done", "y_done"))
        q_sq, q_sum, q_eps, q_pow, q_set = (sem(n) for n in ("q_squared", "q_summed", "q_eps", "q_rsqrt", "qhat_set"))
        k_sq, k_eps, k_pow, k_set = (sem(n) for n in ("k_squared", "k_eps", "k_rsqrt", "khat_set"))
        vhi_set, vlo_set, qT_set, kT_set = (sem(n) for n in ("v_hi_set", "v_lo_set", "qT_set", "kT_set"))
        max_set, exp_set, inv_set, p_set = (sem(n) for n in ("max_set", "exp_set", "inv_set", "p_set"))
        pThi_set, pTlo_set, oThi_set, oTlo_set, y_added = (sem(n) for n in ("pT_hi_set", "pT_lo_set", "oT_hi_set", "oT_lo_set", "y_added"))

        f_x2, f_stats, f_mom, f_eps, f_pow, f_h, f_abs, f_out = (sem(n) for n in (
            "f_x2_in", "f_stats", "f_moments", "f_eps", "f_rstd", "f_h_set", "f_abs_set", "f_out"))
        f_t, f_thi, f_tlo, f_w_hi, f_w_lo, f_bias = (sem(n) for n in (
            "f_transposed", "f_hT_hi", "f_hT_lo", "f_w_hi", "f_w_lo", "f_bias_in"))
        g1_done, g2_done, f_act, f_ahi, f_alo, f_yadd = (sem(n) for n in (
            "up_done", "down_done", "act_set", "act_hi_set", "act_lo_set", "expert_added"))
        r_sum, r_lgt, r_exp, r_top, r_pick, r_gate, r_hg, chain = (sem(n) for n in (
            "router_sums", "router_logits", "router_exp", "router_top", "router_picked", "gates_set", "router_dots", "dve_chain"))

        def wait(eng, s, value):
            if not isinstance(value, int) or value > 0:
                eng.wait_ge(s, value)

        def slot_count(b, j):
            first, second = (32 if k in (4, 5) else 16 for k in (j % RING, j % RING + RING))
            return b * (first + second) + (first if j < RING else first + second)

        def w_piece(t, par, j):
            return t[:, par * WCOLS + j * PIECE:par * WCOLS + (j + 1) * PIECE]

        def wq_at(t, par, c):
            return w_piece(t, par, c)

        def wkv_at(t, par, c):
            return t[:, par * WCOLS + 2048 + c * 256:par * WCOLS + 2048 + (c + 1) * 256]

        def wo_at(t, par, h):
            return w_piece(t, par, 6 + h)

        def kvt_cell(t, par, cell):
            if isinstance(cell, int):
                v = t[:, (par * CELLS + cell) * TILE:(par * CELLS + cell + 1) * TILE]
            else:
                v = t[:, bass.ds(par * CELLS * TILE + cell * TILE, TILE)]
            return v.rearrange("p (c n) -> p c n", c=CH)

        def prep_dst(t, par, cell, src):
            v = kvt_cell(t, par, cell)
            if src == 1:
                return v[:, :, S:3 * S]
            return v.rearrange("p c (r s) -> p c r s", r=4)[:, :, 0:4:3, :]

        def late_piece(w1_part, w2_part, k):
            if k < FPIECES:
                return w1_part[:, k * PIECE:(k + 1) * PIECE]
            return w2_part[:, (FEARLY + k - FPIECES) * PIECE:(FEARLY + k - FPIECES + 1) * PIECE]

        def as_fp32(a):
            return a.bitcast(fp32)

        def bank_rows(b, src):
            v = b[:, :].rearrange("p (c t) -> p c t", c=CH)
            return v if src == 1 else v.rearrange("p c (b s) -> p c b s", b=NB)

        block = es.enter_context(nc.Block())

        @block.sync
        def _(sp):
            def load_piece(b, g, j):
                wait(sp, w_lo_set, b * PIECES + j - RING + 1 if not isinstance(b, int) or b * PIECES + j >= RING else 0)
                dst = raw[:, j % RING, :]
                if j < 4:
                    sp.dma_start(dst, wq_v[:, j, bass.ds(g * GRP * HD, PIECE)]).then_inc(ld[j % RING], 16)
                elif j < 6:
                    kv = dst.rearrange("p (c k n) -> p c k n", c=2, k=2)
                    c = 2 * (j - 4)
                    sp.dma_start(kv[:, :, 0, :], wk_v[:, c:c + 2, bass.ds(g * HD, HD)]).then_inc(ld[j % RING], 16)
                    sp.dma_start(kv[:, :, 1, :], wv_v[:, c:c + 2, bass.ds(g * HD, HD)]).then_inc(ld[j % RING], 16)
                else:
                    sp.dma_start(dst, wo_v[:, g * GRP + j - 6, :] if isinstance(g, int) else
                                 wo_v[:, bass.ds(g * GRP + j - 6, 1), :].rearrange("p a n -> p (a n)")).then_inc(ld[j % RING], 16)

            def load_rows(p, cell):
                wait(sp, xn_set, p)
                sp.dma_start(xrow[:, :], x_rows[:, bass.ds(cell, 1), :].rearrange("p a d -> p (a d)")).then_inc(xrow_in, 16)
                wait(sp, ctx_t, p)
                sp.dma_start(crow[:, :], c_rows[:, bass.ds(cell, 1), :].rearrange("p a d -> p (a d)")).then_inc(crow_in, 16)

            load_rows(0, 0)
            sp.dma_start(cst[:, :], consts).then_inc(s_cst, 16)
            for k, a in enumerate((g_xattn, g_ffn)):
                sp.dma_start(small[:, k:k + 1], a.partition_broadcast(P)).then_inc(s_par, 16)
            for k, a in enumerate((qnw, knw)):
                sp.dma_start(small[:, 4 + k:5 + k], a.rearrange("(p a) -> p a", a=1)).then_inc(s_par, 16)
            at = 0
            for p in range(CELLS):
                if p:
                    load_rows(p, p)
                for j in SPLITS[p]:
                    load_piece(0, 0, j)
                    at += 1
            for par in range(2):
                sp.dma_start(y[:, par * CELLS:(par + 1) * CELLS, :],
                             x_rows[:, par * CELLS:(par + 1) * CELLS, :]).then_inc(y_next, 16)
            load_rows(CELLS, CELLS)
            for j in range(PIECES):
                load_piece(1, 1, j)

            def iteration_loads(q, gp):
                it = q * ITS + gp
                wrap = isinstance(gp, int) and gp == ITS - 1
                for j in range(PIECES):
                    load_piece(it * 2 + 2, 0 if wrap else gp * 2 + 2, j)
                for j in range(PIECES):
                    load_piece(it * 2 + 3, 1 if wrap else gp * 2 + 3, j)
                cell = it + CELLS + 1
                load_rows(cell, sp.snap(cell % (CELLS * QUARTERS)))

            iteration_loads(0, 0)
            def quarter_loads(q):
                with sp.Fori(1, ITS - 1) as gp:
                    iteration_loads(q, gp)
                iteration_loads(q, ITS - 1)
                iteration_loads(q + 1, 0)

            with sp.Fori(0, QUARTERS - 2) as q:
                quarter_loads(q)
                done = y[:, bass.ds(sp.snap((q % 2) * CELLS), CELLS), :]
                coming = sp.snap((q + 2) * CELLS)
                sp.wait_ge(y_added, (q + 1) * (STEPS * ITS) + 3)
                sp.dma_start(x2_rows[:, bass.ds(q * CELLS, CELLS), :], done).then_inc(x2_out, 16)
                sp.wait_ge(x2_out, (q + 1) * 16)
                sp.dma_start(done, x_rows[:, bass.ds(coming, CELLS), :]).then_inc(y_next, 16)
            quarter_loads(QUARTERS - 2)
            with sp.Fori(1, ITS - 1) as gp:
                iteration_loads(QUARTERS - 1, gp)

            for j in range(FEARLY):
                sp.wait_ge(w_lo_set, 2 * NIT * PIECES + j - RING + 1)
                halves = 2 if j in (4, 5) else 1
                for k in range(halves):
                    cols = slice(k * PIECE // halves, (k + 1) * PIECE // halves)
                    sp.dma_start(raw[:, j % RING, cols], w2_v[:, j, cols]).then_inc(ld[j % RING], 16)
            for k in range(FLATE):
                if k < RING:
                    sp.wait_ge(w_lo_set, (2 * NIT + 1) * PIECES + k - RING + 1)
                else:
                    sp.wait_ge(f_w_lo, k - RING + 1)
                sp.dma_start(raw[:, k % RING, :], w1_v[:, k, :] if k < FPIECES else w2_v[:, FEARLY + k - FPIECES, :]).then_inc(ld[k % RING], 16)
                if k == RING - 1:
                    sp.wait_ge(ctx_t, NIT + CELLS)
                    sp.dma_start(gw_all, gate_w[0:D, :].rearrange("d e -> (d e)").partition_broadcast(P)).then_inc(f_bias, 16)
                    sp.dma_start(gwl[:, :], gate_w[D:D + 1, :].rearrange("d e -> (d e)").partition_broadcast(P)).then_inc(f_bias, 16)
                    sp.dma_start(gb[:, :], gate_b.partition_broadcast(P)).then_inc(f_bias, 16)
                    sp.dma_start(b1_sb[:, :], b1).then_inc(f_bias, 16)
            sp.wait_ge(s_done, NCELL + 1)
            sp.dma_start(b2_all, b2.rearrange("e d -> (e d)").partition_broadcast(P)).then_inc(f_bias, 16)
            sp.wait_ge(y_next, QUARTERS * 16)
            for T in range(QUARTERS):
                half_y = y[:, T % 2 * CELLS:(T % 2 + 1) * CELLS, :]
                out_c = (T + 2) % QUARTERS * CELLS
                for c in range(CELLS):
                    sp.wait_ge(f_yadd, T * NE * CELLS + (NE - 1) * CELLS + c + 1)
                    sp.dma_start(o_rows[:, out_c + c, :], half_y[:, c, :]).then_inc(f_out, 16)
                if T + 2 < QUARTERS:
                    sp.wait_ge(f_out, (T + 1) * CELLS * 16)
                    sp.dma_start(half_y, x2_rows[:, T * CELLS:(T + 1) * CELLS, :]).then_inc(f_x2, 16)
            sp.wait_ge(f_out, QUARTERS * CELLS * 16)

        @block.gpsimd
        def _(pool):
            pow_ = lambda out, a, n: nc.gpsimd.tensor_tensor(out, a, half[:, 0:n], ALU.pow)

            def low_piece(b, j):
                pool.wait_ge(w_hi_set, b * PIECES + j + 1)
                par = low_piece.par
                nc.gpsimd.tensor_tensor(w_piece(w_lo, par, j), raw[:, j % RING, :], as_fp32(w_piece(w_hi, par, j)),
                                        ALU.subtract).then_inc(w_lo_set, 1)

            def ln_power(p):
                pool.wait_ge(st_c, p + 1)
                pow_(rstd[:, 0:1], vare[:, 0:1], 1).then_inc(ln_pow, 1)

            pool.wait_ge(s_init, 1)
            low_piece.par = 0
            for p in range(CELLS):
                ln_power(p)
                for j in SPLITS[p]:
                    low_piece(0, j)
            with pool.Fori(0, NIT) as it:
                for s in range(STEPS):
                    i = it * STEPS + s
                    pool.wait_ge(q_eps, i + 1)
                    pow_(ssq[:, 2, :], ssq[:, 1, :], GRP).then_inc(q_pow, 1)
                    low_piece.par = 1 - s // CELLS
                    for j in SPLITS[s % CELLS]:
                        low_piece(it * 2 + s // CELLS + 1, j)
                    pool.wait_ge(k_eps, i + 1)
                    pow_(ssk[:, 2, :], ssk[:, 1, :], NB).then_inc(k_pow, 1)
                    if s == 3:
                        ln_power(it + CELLS)
            def ffn_power(T):
                pool.wait_ge(f_eps, T + 1)
                pow_(rstd[:, :], vare[:, :], CELLS).then_inc(f_pow, 1)

            for k in range(FLATE):
                pool.wait_ge(f_w_hi, k + 1)
                nc.gpsimd.tensor_tensor(late_piece(w1_lo, w2_lo, k), raw[:, k % RING, :], as_fp32(late_piece(w1_hi, w2_hi, k)),
                                        ALU.subtract).then_inc(f_w_lo, 1)
                if k == 8:
                    ffn_power(0)
            with pool.Fori(1, QUARTERS + 1) as T:
                ffn_power(T)

        @block.scalar
        def _(act_e):
            def high_piece(b, j, par):
                act_e.wait_ge(ld[j % RING], slot_count(b, j))
                nc.scalar.activation(w_piece(w_hi, par, j), raw[:, j % RING, :], ACT.Copy).then_inc(w_hi_set, 1)

            def q_part(i):
                act_e.wait_ge(q_done, i + 1)
                nc.scalar.activation(sq[:, :, :].rearrange("p g d -> p (g d)"), ps_q[:, :], ACT.Square).then_inc(q_sq, 1)

            def p_high(m):
                act_e.wait_ge(tp_done, m + 3)
                nc.scalar.activation(pT_hi[:, :, :].rearrange("p b r -> p (b r)"), ps_tp[:, :], ACT.Copy).then_inc(pThi_set, 1)

            def o_high(m):
                act_e.wait_ge(o_done, m + 3)
                nc.scalar.activation(oT_hi[:, :, :, :], ps_o[:, :].rearrange("p (b g s) -> p g b s", b=NB, g=GRP),
                                     ACT.Copy).then_inc(oThi_set, 1)

            def q_turned(m):
                act_e.wait_ge(tqk_done, m + 2)
                nc.scalar.activation(qT[:, :, :, :], ps_tq[:, :].rearrange("p (g b s) -> p b g s", g=GRP, b=NB),
                                     ACT.Copy).then_inc(qT_set, 1)

            def kv_part(i, s):
                act_e.wait_ge(kv_done, i + 1)
                kv = ps_kv[:, :].rearrange("p (b k d) -> p b k d", b=NB, k=2)
                for b in range(NB):
                    last = nc.scalar.activation(sqk[:, b, :], kv[:, b, 0, :], ACT.Square, accum_out=ssk[:, 0, b:b + 1])
                last.then_inc(k_sq, 1)
                nc.scalar.activation(v_hi[:, s % 2, :, :], kv[:, :, 1, :], ACT.Copy, scale=tanh_x).then_inc(vhi_set, 1)

            def softmax(m):
                act_e.wait_ge(max_set, m + 2)
                for r in range(GRP):
                    last = nc.scalar.activation(prob[:, r, :], ps_s[:, r * HD:(r + 1) * HD], ACT.Exp,
                                                bias=nmax[:, r:r + 1], accum_out=rsum[:, r:r + 1])
                last.then_inc(exp_set, 1)

            act_e.wait_ge(s_par, 64)
            nc.scalar.activation(small[:, 2:4], small[:, 0:2], ACT.Tanh).then_inc(s_tanh, 1)
            for p in range(CELLS):
                for j in SPLITS[p]:
                    high_piece(0, j, 0)
            act_e.wait_ge(s_tanh, 1)
            with act_e.Fori(0, NIT) as it:
                for s in range(STEPS):
                    i = it * STEPS + s
                    p_high(i - 2)
                    q_part(i)
                    if s % CELLS == 2:
                        act_e.wait_ge(y_done, i)
                    for j in SPLITS[s % CELLS]:
                        high_piece(it * 2 + s // CELLS + 1, j, 1 - s // CELLS)
                    o_high(i - 2)
                    q_turned(i - 1)
                    kv_part(i, s)
                    softmax(i - 1)
            def late_high(k):
                act_e.wait_ge(ld[k % RING], slot_count(2 * NIT, PIECES - RING + k % RING) + 16 * (k // RING + 1))
                nc.scalar.activation(late_piece(w1_hi, w2_hi, k), raw[:, k % RING, :], ACT.Copy).then_inc(f_w_hi, 1)

            act_e.wait_ge(ctx_lo, NIT + CELLS)
            late_high(0)
            late_high(1)
            p_high(NCELL - 2)
            for k in range(2, 5):
                late_high(k)
            o_high(NCELL - 2)
            q_turned(NCELL - 1)
            for k in range(5, 8):
                late_high(k)
            softmax(NCELL - 1)
            for k in range(8, 11):
                late_high(k)
            p_high(NCELL - 1)
            late_high(11)
            o_high(NCELL - 1)
            for k in range(12, FLATE):
                late_high(k)

            def turned_high(T):
                for c in range(CELLS):
                    act_e.wait_ge(f_t, T * CELLS + c + 1)
                    nc.scalar.activation(hT_hi[:, :, c * P:(c + 1) * P], banks[c][:, :].rearrange("p (c t) -> p c t", c=CH),
                                         ACT.Copy).then_inc(f_thi, 1)

            def strengths(T):
                for c in range(CELLS):
                    last = nc.scalar.activation(act[:, c % 2, :], h[:, c, :], ACT.Abs, accum_out=asum[:, c:c + 1])
                    if c % 2:
                        last.then_inc(f_abs, 1)
                        act_e.wait_ge(f_abs, T * 2 + c // 2 + 1)

            turned_high(0)
            strengths(0)
            act_e.wait_ge(f_bias, 80)
            with act_e.Fori(0, QUARTERS) as T:
                act_e.wait_ge(r_lgt, T + 1)
                nc.scalar.activation(r3[:, 2, :, :], r3[:, 1, :, :], ACT.Exp).then_inc(r_exp, 1)
                for e, func in enumerate((ACT.Tanh, ACT.Gelu, ACT.Silu)):
                    for f in range(CH):
                        k = T * (NE * CH) + e * CH + f
                        act_e.wait_ge(g1_done, k + 1)
                        if e or f >= 2:
                            act_e.wait_ge(f_alo, k - 1)
                        nc.scalar.activation(act[:, f % 2, :], banks[f][:, :], func,
                                             bias=b1_sb[:, e * CH + f:e * CH + f + 1]).then_inc(f_act, 1)
                turned_high(T + 1)
                act_e.wait_ge(f_alo, T * (NE * CH) + NE * CH)
                strengths(T + 1)

        @block.vector
        def _(dve):
            V = nc.vector

            def moments(n, summed, squared, done, count):
                stat = bnst[:, 0:n, :].rearrange("p c (k t) -> p c k t", k=2)
                dve.wait_ge(summed, count + 1)
                V.tensor_tensor(mom[:, 0, 0:n], stat[:, :, 0, 1], stat[:, :, 1, 1], ALU.add)
                V.tensor_tensor(mom[:, 1, 0:n], stat[:, :, 0, 1], stat[:, :, 1, 1], ALU.subtract)
                V.tensor_tensor(mom[:, 2, 0:n], stat[:, :, 0, 2], stat[:, :, 1, 2], ALU.add).then_inc(squared, 1)
                dve.wait_ge(squared, 2 * count + 1)
                V.tensor_scalar(mean[:, 0:n], mom[:, 0, 0:n], 0.5, None, ALU.mult)
                V.tensor_scalar(mom[:, 3, 0:n], mom[:, 2, 0:n], 1.0 / D, LN_EPS, ALU.mult, ALU.add)
                V.tensor_tensor(mom[:, 4, 0:n], mom[:, 1, 0:n], mom[:, 1, 0:n], ALU.mult).then_inc(squared, 1)
                dve.wait_ge(squared, 2 * count + 2)
                V.scalar_tensor_tensor(vare[:, 0:n], mom[:, 4, 0:n], 0.25, mom[:, 3, 0:n], ALU.mult, ALU.add).then_inc(done, 1)

            def ln_stats(p):
                dve.wait_ge(xrow_in, p * 16 + 16)
                V.bn_stats(bnst[:, 0, :], xrow).then_inc(st_a, 1)
                moments(1, st_a, st_b, st_c, p)

            def ln_apply(p):
                dve.wait_ge(ln_pow, p + 1)
                V.tensor_scalar(xn, xrow, mean[:, 0:1], rstd[:, 0:1], ALU.subtract, ALU.mult).then_inc(xn_set, 1)

            def rows_turned(p, par, cell, src):
                turned, hi_set, lo_set = ((ctx_t, ctx_hi, ctx_lo), (lat_t, lat_hi, lat_lo))[src]
                dst_hi, dst_lo = prep_dst(kvt_hi, par, cell, src), prep_dst(kvt_lo, par, cell, src)
                dve.wait_ge(turned, p + 1)
                V.tensor_scalar(dst_hi, bank_rows(ps_tq, src), 1.0, None, ALU.mult).then_inc(hi_set, 1)
                dve.wait_ge(hi_set, p + 1)
                V.tensor_tensor(dst_lo, bank_rows(ps_tq, src), as_fp32(dst_hi), ALU.subtract).then_inc(lo_set, 1)

            def scale_q(i, s):
                dve.wait_ge(q_pow, i + 1)
                V.tensor_tensor(qhat[:, s % 2, :, :], ps_q[:, :].rearrange("p (g d) -> p g d", g=GRP),
                                ssq[:, 2, :].unsqueeze(2).to_broadcast([P, GRP, HD]), ALU.mult).then_inc(q_set, 1)

            def sum_q(i):
                dve.wait_ge(q_sq, i + 1)
                V.tensor_reduce(ssq[:, 0, :], sq[:, :, :], AX.X, ALU.add).then_inc(q_sum, 1)
                dve.wait_ge(q_sum, i + 1)
                V.tensor_scalar(ssq[:, 1, :], ssq[:, 0, :], RMS_EPS * HD, None, ALU.add).then_inc(q_eps, 1)

            def p_low(m):
                dve.wait_ge(pThi_set, m + 3)
                V.tensor_tensor(pT_lo[:, :, :].rearrange("p b r -> p (b r)"), ps_tp[:, :],
                                as_fp32(pT_hi[:, :, :]).rearrange("p b r -> p (b r)"), ALU.subtract).then_inc(pTlo_set, 1)

            def o_low(m):
                dve.wait_ge(oThi_set, m + 3)
                V.tensor_tensor(oT_lo[:, :, :, :], ps_o[:, :].rearrange("p (b g s) -> p g b s", b=NB, g=GRP),
                                as_fp32(oT_hi[:, :, :, :]), ALU.subtract).then_inc(oTlo_set, 1)

            def k_turned(m):
                dve.wait_ge(tqk_done, m + 2)
                V.tensor_scalar(kT[:, :, :].rearrange("p b k -> p (b k)"), ps_tk[:, 0:NB * HD], kw, None, ALU.mult).then_inc(kT_set, 1)

            def k_sum_v_low(i, s):
                dve.wait_ge(k_sq, i + 1)
                V.tensor_scalar(ssk[:, 1, :], ssk[:, 0, :], RMS_EPS * HD, None, ALU.add).then_inc(k_eps, 1)
                kv = ps_kv[:, :].rearrange("p (b k d) -> p b k d", b=NB, k=2)
                dve.wait_ge(vhi_set, i + 1)
                V.scalar_tensor_tensor(v_lo[:, s % 2, :, :], kv[:, :, 1, :], tanh_x, as_fp32(v_hi[:, s % 2, :, :]),
                                       ALU.mult, ALU.subtract).then_inc(vlo_set, 1)

            def row_max(m):
                dve.wait_ge(s_done, m + 2)
                V.tensor_reduce(nmax[:, :], ps_s[:, :].rearrange("p (r k) -> p r k", r=GRP), AX.X, ALU.max,
                                negate=True).then_inc(max_set, 1)

            def scale_k(i):
                dve.wait_ge(k_pow, i + 1)
                kv = ps_kv[:, :].rearrange("p (b k d) -> p b k d", b=NB, k=2)
                V.tensor_tensor(khat[:, :, :], kv[:, :, 0, :], ssk[:, 2, :].unsqueeze(2).to_broadcast([P, NB, HD]),
                                ALU.mult).then_inc(k_set, 1)

            def normalise(m):
                dve.wait_ge(exp_set, m + 2)
                V.reciprocal(rinv[:, :], rsum[:, :]).then_inc(inv_set, 1)
                dve.wait_ge(inv_set, m + 2)
                V.tensor_tensor(prob[:, :, :], prob[:, :, :], rinv[:, :].unsqueeze(2).to_broadcast([P, GRP, HD]),
                                ALU.mult).then_inc(p_set, 1)

            def add_y(m, c):
                dve.wait_ge(y_done, m + 3)
                slot = (m + 2 * STEPS * ITS) // (STEPS * ITS) % 2 * CELLS + c
                yt = y[:, slot, :] if isinstance(slot, int) else y[:, bass.ds(slot, 1), :].rearrange("p a d -> p (a d)")
                V.tensor_tensor(yt, ps_y[:, :], yt, ALU.add).then_inc(y_added, 1)

            V.memset(as_fp32(v_hi[:, :, :, :]).rearrange("p k b d -> p (k b d)"), 0.0)
            V.memset(as_fp32(v_lo[:, :, :, :]).rearrange("p k b d -> p (k b d)"), 0.0).then_inc(vlo_set, 1)
            V.memset(as_fp32(w_hi[:, WCOLS + 6 * PIECE:2 * WCOLS]), 0.0)
            V.memset(as_fp32(w_lo[:, WCOLS + 6 * PIECE:2 * WCOLS]), 0.0).then_inc(y_added, 1)
            V.memset(qhat[:, 1, :, :].rearrange("p g d -> p (g d)"), 0.0).then_inc(q_set, 1)
            V.memset(khat[:, :, :].rearrange("p b d -> p (b d)"), 0.0).then_inc(k_set, 1)
            V.memset(prob[:, :, :].rearrange("p g d -> p (g d)"), 0.0).then_inc(p_set, 1)
            V.memset(hg[:, :, :], 0.0).then_inc(f_x2, 1)
            V.memset(half[:, :], -0.5).then_inc(s_init, 1)
            dve.wait_ge(s_par, 64)
            V.tensor_tensor(small[:, 7:8], small[:, 4:5], small[:, 5:6], ALU.mult).then_inc(s_prod, 1)
            dve.wait_ge(s_prod, 1)
            V.tensor_scalar(kw, small[:, 7:8], float(HD) ** 0.5, None, ALU.mult).then_inc(s_kw, 1)
            dve.wait_ge(s_kw, 1)
            dve.wait_ge(s_tanh, 1)
            for p in range(CELLS):
                ln_stats(p)
                ln_apply(p)
                rows_turned(p, 0, p, 1)
                rows_turned(p, 0, p, 0)
            dve.wait_ge(y_next, 32)
            with dve.Fori(0, NIT) as it:
                for s in range(STEPS):
                    i = it * STEPS + s
                    p = it + CELLS
                    p_low(i - 2)
                    sum_q(i)
                    k_turned(i - 1)
                    scale_q(i, s)
                    o_low(i - 2)
                    k_sum_v_low(i, s)
                    row_max(i - 1)
                    scale_k(i)
                    normalise(i - 1)
                    if s in (5, 6):
                        rows_turned(p, 0, (it // ITS + 1) % 2 * CELLS + it % ITS, 6 - s)
                    if s == 0:
                        dve.wait_ge(y_next, it // ITS * 16 + 16)
                    add_y(i - 2, (s - 2) % CELLS)
                    if s == 3:
                        ln_stats(p)
                    if s == 4:
                        ln_apply(p)
            def ffn_stats(rows, cells):
                for c in cells:
                    last = V.bn_stats(bnst[:, c, :], rows[:, c, :])
                return last

            def ffn_normalise(T, rows):
                dve.wait_ge(f_pow, T + 1)
                for c in range(CELLS):
                    V.tensor_scalar(h[:, c, :], rows[:, c, :], mean[:, c:c + 1], rstd[:, c:c + 1], ALU.subtract, ALU.mult).then_inc(f_h, 1)

            def turned_low(T):
                for c in range(CELLS):
                    dve.wait_ge(f_thi, T * CELLS + c + 1)
                    V.tensor_tensor(hT_lo[:, :, c * P:(c + 1) * P], banks[c][:, :].rearrange("p (c t) -> p c t", c=CH),
                                    as_fp32(hT_hi[:, :, c * P:(c + 1) * P]), ALU.subtract).then_inc(f_tlo, 1)

            def router_dots(T, c):
                for e in range(NE):
                    V.tensor_tensor_reduce(out=rjunk, in0=h[:, c, :], in1=gw_sb[:, :, e], scale=1.0, scalar=0.0,
                                           op0=ALU.mult, op1=ALU.add, accum_out=hg[:, c, e:e + 1]).then_inc(r_hg, 1)
                    dve.wait_ge(r_hg, T * (CELLS * NE) + c * NE + e + 1)

            halves = [y[:, par * CELLS:(par + 1) * CELLS, :] for par in range(2)]
            p_low(NCELL - 2)
            ffn_stats(halves[0], (0, 1))
            k_turned(NCELL - 1)
            o_low(NCELL - 2)
            ffn_stats(halves[0], (2, 3)).then_inc(f_stats, 1)
            row_max(NCELL - 1)
            moments(CELLS, f_stats, f_mom, f_eps, 0)
            add_y(NCELL - 2, CELLS - 2)
            normalise(NCELL - 1)
            p_low(NCELL - 1)
            o_low(NCELL - 1)
            dve.wait_ge(f_w_lo, FLATE)
            ffn_normalise(0, halves[0])
            add_y(NCELL - 1, CELLS - 1)

            turned_low(0)
            dve.wait_ge(f_bias, 80)
            for c in range(CELLS):
                router_dots(0, c)

            def ffn_group(j, par):
                T = j * 2 + par
                mine, coming = halves[par], halves[1 - par]
                links = [0]

                def link(ins):
                    links[0] += 1
                    ins.then_inc(chain, 1)
                    dve.wait_ge(chain, T * CHAIN + links[0])

                def split_act(e, f):
                    k = T * (NE * CH) + e * CH + f
                    dve.wait_ge(f_act, k + 1)
                    V.tensor_copy(a_hi[:, e % 2, f, :], act[:, f % 2, :]).then_inc(f_ahi, 1)
                    dve.wait_ge(f_ahi, k + 1)
                    V.tensor_tensor(a_lo[:, e % 2, f, :], act[:, f % 2, :], as_fp32(a_hi[:, e % 2, f, :]),
                                    ALU.subtract).then_inc(f_alo, 1)

                def add_expert(e, c):
                    n = T * (NE * CELLS) + e * CELLS + c
                    dve.wait_ge(g2_done, n + 1)
                    if e:
                        dve.wait_ge(f_yadd, n - CELLS + 1)
                    V.scalar_tensor_tensor(mine[:, c, :], banks[4 + c][:, :], gate[:, c, e:e + 1], mine[:, c, :],
                                           ALU.mult, ALU.add).then_inc(f_yadd, 1)

                bc = lambda a: a.unsqueeze(2).to_broadcast([P, CELLS, NE])
                be = lambda a: a.unsqueeze(1).to_broadcast([P, CELLS, NE])
                dve.wait_ge(r_sum, T + 1)
                V.tensor_scalar(rt[:, 0, :], banks[4][:, 0:CELLS], 1.0 / ((S - VIS) * D), None, ALU.mult)
                link(V.tensor_scalar(rt[:, 1, :], banks[4][:, CELLS:2 * CELLS], 1.0 / (VIS * D), 1e-8, ALU.mult, ALU.add))
                link(V.reciprocal(rt[:, 2, :], rt[:, 1, :]))
                link(V.tensor_tensor(rt[:, 3, :], rt[:, 0, :], rt[:, 2, :], ALU.mult))
                link(V.tensor_tensor(r3[:, 0, :, :], bc(rt[:, 3, :]), be(gwl[:, :]), ALU.mult))
                link(V.tensor_tensor(r3[:, 3, :, :], r3[:, 0, :, :], hg[:, :, :], ALU.add))
                link(V.tensor_tensor(r3[:, 4, :, :], r3[:, 3, :, :], be(gb[:, :]), ALU.add))
                link(V.tensor_reduce(rt[:, 4, :], r3[:, 4, :, :], AX.X, ALU.max))
                V.tensor_tensor(r3[:, 1, :, :], r3[:, 4, :, :], bc(rt[:, 4, :]), ALU.subtract).then_inc(r_lgt, 1)
                dve.wait_ge(r_exp, T + 1)
                link(V.tensor_reduce(rt[:, 5, :], r3[:, 2, :, :], AX.X, ALU.add))
                link(V.reciprocal(rt[:, 6, :], rt[:, 5, :]))
                score = r3[:, 5, :, :]
                link(V.tensor_tensor(score, r3[:, 2, :, :], bc(rt[:, 6, :]), ALU.mult))
                s0, s1, s2 = (r3[:, 5, :, e] for e in range(NE))
                c01, c02, c12 = rt[:, 7, :], rt[:, 8, :], rt[:, 9, :]
                V.tensor_tensor(c01, s0, s1, ALU.is_ge)
                V.tensor_tensor(c02, s0, s2, ALU.is_ge)
                link(V.tensor_tensor(c12, s1, s2, ALU.is_ge))
                rank = r3[:, 6, :, :]
                V.tensor_tensor(rt[:, 10, :], c01, c02, ALU.add)
                V.tensor_tensor(rt[:, 11, :], c01, c12, ALU.subtract)
                link(V.tensor_tensor(r3[:, 6, :, 2], c02, c12, ALU.add))
                V.tensor_scalar(r3[:, 6, :, 0], rt[:, 10, :], -1.0, 2.0, ALU.mult, ALU.add)
                link(V.tensor_scalar(r3[:, 6, :, 1], rt[:, 11, :], 1.0, None, ALU.add))
                V.tensor_scalar(pick[:, 0, :, :], rank, 0.0, None, ALU.is_equal)
                V.tensor_scalar(pick[:, 1, :, :], rank, 1.0, None, ALU.is_equal).then_inc(r_top, 1)
                dve.wait_ge(r_top, T + 1)
                V.tensor_reduce(rt[:, 12, :], score, AX.X, ALU.max)
                link(V.tensor_tensor(r3[:, 7, :, :], score, pick[:, 1, :, :], ALU.mult))
                link(V.tensor_reduce(rt[:, 13, :], r3[:, 7, :, :], AX.X, ALU.add))
                link(V.scalar_tensor_tensor(rt[:, 14, :], rt[:, 12, :], 1e-8, rt[:, 13, :], ALU.add, ALU.add))
                link(V.reciprocal(rt[:, 15, :], rt[:, 14, :]))
                link(V.tensor_scalar(rt[:, 16, :], rt[:, 15, :], tanh_f, None, ALU.mult))
                V.tensor_tensor(rt[:, 17, :], rt[:, 12, :], rt[:, 16, :], ALU.mult)
                link(V.tensor_tensor(rt[:, 18, :], rt[:, 13, :], rt[:, 16, :], ALU.mult))

                for f in range(CH):
                    split_act(0, f)
                dve.wait_ge(r_pick, T + 1)
                picked = banks[4][:, 0:2 * CELLS * NE].rearrange("p (k c e) -> p k c e", k=2, c=CELLS)
                V.tensor_tensor(r3[:, 0, :, :], picked[:, 0, :, :], bc(rt[:, 17, :]), ALU.mult)
                link(V.tensor_tensor(r3[:, 3, :, :], picked[:, 1, :, :], bc(rt[:, 18, :]), ALU.mult))
                V.tensor_tensor(gate[:, :, :], r3[:, 0, :, :], r3[:, 3, :, :], ALU.add).then_inc(r_gate, 1)
                dve.wait_ge(r_gate, T + 1)
                for e in range(NE):
                    for c in range(CELLS):
                        last = V.scalar_tensor_tensor(mine[:, c, :], b2_sb[:, e, :], gate[:, c, e:e + 1], mine[:, c, :], ALU.mult, ALU.add)
                    link(last)
                for f in range(CH):
                    split_act(1, f)
                for c in range(CELLS):
                    add_expert(0, c)
                dve.wait_ge(f_x2, 17 if par else j * 32 + 1)
                ffn_stats(coming, range(CELLS)).then_inc(f_stats, 1)
                moments(CELLS, f_stats, f_mom, f_eps, T + 1)
                dve.wait_ge(f_abs, T * 2 + 2)
                ffn_normalise(T + 1, coming)
                for f in range(CH):
                    split_act(2, f)
                for c in range(CELLS):
                    add_expert(1, c)
                turned_low(T + 1)
                for c in range(CELLS):
                    router_dots(T + 1, c)
                    add_expert(2, c)
                assert links[0] == CHAIN, links

            with dve.Fori(0, QUARTERS // 2) as j:
                for par in range(2):
                    ffn_group(j, par)

        @block.tensor
        def _(pe):
            mm = nc.tensor.matmul

            def split_product(out, pairs, before_last=None):
                n = len(pairs)
                for k, (a_hi_, a_lo_, b_hi_, b_lo_) in enumerate(pairs):
                    if before_last is not None and k == n - 1:
                        before_last()
                    mm(out, a_hi_, b_hi_, start=k == 0, stop=False)
                    mm(out, a_hi_, b_lo_, start=False, stop=False)
                    last = mm(out, a_lo_, b_hi_, start=False, stop=k == n - 1)
                return last

            def turn(p, src):
                if src == 1:
                    pe.wait_ge(xn_set, p + 1)
                    rows, done = xn, lat_t
                else:
                    pe.wait_ge(crow_in, p * 16 + 16)
                    rows, done = crow, ctx_t
                for c in range(CH):
                    last = nc.tensor.transpose(ps_tq[:, c * P:(c + 1) * P], rows[:, c * P:(c + 1) * P], ident)
                last.then_inc(done, 1)

            def project_q(m, kpar, cell, wpar):
                hi, lo = kvt_cell(kvt_hi, kpar, cell), kvt_cell(kvt_lo, kpar, cell)
                return split_product(ps_q[:, :], [(hi[:, c, S:3 * S], lo[:, c, S:3 * S], wq_at(w_hi, wpar, c), wq_at(w_lo, wpar, c))
                                                  for c in range(CH)], before_last=lambda: turn_p(m))

            def project_kv(b, kpar, cell, wpar):
                hi, lo = kvt_cell(kvt_hi, kpar, cell), kvt_cell(kvt_lo, kpar, cell)
                rows = lambda t, c: t[:, c, b * 2 * S:(b + 1) * 2 * S]
                return split_product(ps_kv[:, b * 2 * HD:(b + 1) * 2 * HD], [
                    (rows(hi, c), rows(lo, c), wkv_at(w_hi, wpar, c), wkv_at(w_lo, wpar, c)) for c in range(CH)])

            def turn_p(m):
                pe.wait_ge(p_set, m + 3)
                for r in range(GRP):
                    last = nc.tensor.transpose(ps_tp[:, r * P:(r + 1) * P], prob[:, r, :], ident)
                last.then_inc(tp_done, 1)

            def weigh_v(m, s):
                pe.wait_ge(pTlo_set, m + 3)
                for b in range(NB):
                    k = s % 2
                    last = split_product(ps_o[:, b * GRP * S:(b + 1) * GRP * S], [
                        (v_hi[:, k, b, :], v_lo[:, k, b, :], pT_hi[:, b, :], pT_lo[:, b, :])])
                last.then_inc(o_done, 1)

            def turn_qk(m, s):
                for g in range(GRP):
                    nc.tensor.transpose(ps_tq[:, g * P:(g + 1) * P], qhat[:, s % 2, g, :], ident)
                for b in range(NB):
                    last = nc.tensor.transpose(ps_tk[:, b * P:(b + 1) * P], khat[:, b, :], ident)
                last.then_inc(tqk_done, 1)

            def scores(m):
                pe.wait_ge(qT_set, m + 2)
                pe.wait_ge(kT_set, m + 2)
                for r in range(GRP):
                    b, g = r // 2, r % 2 * 2
                    last = mm(ps_s[:, r * HD:(r + 1) * HD], qT[:, b, g:g + 2, :].rearrange("p g s -> p (g s)"), kT[:, b, :],
                              start=True, stop=True)
                last.then_inc(s_done, 1)

            def project_o(m, wpar):
                pe.wait_ge(oTlo_set, m + 3)
                flat = lambda t, h: t[:, h, :, :].rearrange("p b s -> p (b s)")
                split_product(ps_y[:, :], [(flat(oT_hi, h), flat(oT_lo, h), wo_at(w_hi, wpar, h), wo_at(w_lo, wpar, h))
                                           for h in range(GRP)]).then_inc(y_done, 1)

            pe.wait_ge(s_cst, 16)
            for p in range(CELLS):
                if p:
                    pe.wait_ge(ctx_lo, p)
                turn(p, 1)
                pe.wait_ge(lat_lo, p + 1)
                turn(p, 0)
            with pe.Fori(0, QUARTERS // 2) as j:
                for kpar in range(2):
                    with pe.Fori(0, ITS) as gp:
                        it = (j * 2 + kpar) * ITS + gp
                        pe.wait_ge(ctx_lo, (j * 2 + kpar) * CELLS + CELLS)
                        for s in range(STEPS):
                            i, blk, cell, wpar = it * STEPS + s, it * 2 + s // CELLS, s % CELLS, s // CELLS
                            if cell == 0:
                                pe.wait_ge(w_lo_set, blk * PIECES + 4)
                            pe.wait_ge(q_set, i + 1)
                            project_q(i - 2, kpar, cell, wpar).then_inc(q_done, 1)
                            if cell == 0:
                                pe.wait_ge(w_lo_set, blk * PIECES + 6)
                            pe.wait_ge(vlo_set, i + 1)
                            pe.wait_ge(k_set, i + 1)
                            project_kv(0, kpar, cell, wpar)
                            weigh_v(i - 2, s)
                            if s == 0:
                                pe.wait_ge(ctx_lo, it + CELLS)
                            if s == 6:
                                pe.wait_ge(lat_lo, it + CELLS + 1)
                            if s == 7:
                                pe.wait_ge(ctx_lo, it + CELLS + 1)
                            turn_qk(i - 1, s - 1)
                            project_kv(1, kpar, cell, wpar).then_inc(kv_done, 1)
                            scores(i - 1)
                            if s in (5, 6):
                                turn(it + CELLS, 6 - s)
                            if cell == 2:
                                pe.wait_ge(w_lo_set, blk * PIECES + PIECES)
                            pe.wait_ge(y_added, i + 1)
                            project_o(i - 2, wpar if cell >= 2 else 1 - wpar)
            pe.wait_ge(q_set, NCELL + 1)
            pe.wait_ge(k_set, NCELL + 1)
            turn_p(NCELL - 2)
            turn_qk(NCELL - 1, 1)
            weigh_v(NCELL - 2, 0)
            scores(NCELL - 1)
            pe.wait_ge(y_added, NCELL + 1)
            project_o(NCELL - 2, 1)
            turn_p(NCELL - 1)
            weigh_v(NCELL - 1, 1)
            pe.wait_ge(y_added, NCELL + 2)
            project_o(NCELL - 1, 1)

            def turn_h(T):
                for c in range(CELLS):
                    pe.wait_ge(f_h, T * CELLS + c + 1)
                    if not isinstance(T, int):
                        pe.wait_ge(f_act, T * (NE * CH) - CH + c + 1)
                    for k in range(CH):
                        last = nc.tensor.transpose(banks[c][:, k * P:(k + 1) * P], h[:, c, k * P:(k + 1) * P], ident)
                    last.then_inc(f_t, 1)

            turn_h(0)
            with pe.Fori(0, QUARTERS) as T:
                def up(e):
                    pe.wait_ge(f_w_lo, (e + 1) * CH)
                    for f in range(CH):
                        k = T * (NE * CH) + e * CH + f
                        if e:
                            pe.wait_ge(f_act, k - CH + 1)
                        at = lambda t, c: t[:, (e * CH + c) * D + f * P:(e * CH + c) * D + (f + 1) * P]
                        split_product(banks[f][:, :], [(at(w1_hi, c), at(w1_lo, c), hT_hi[:, c, :], hT_lo[:, c, :])
                                                       for c in range(CH)]).then_inc(g1_done, 1)
                        if e == 0 and f == 0:
                            strength_sums()

                def strength_sums():
                    pe.wait_ge(f_abs, T * 2 + 2)
                    pe.wait_ge(r_hg, T * (CELLS * NE) + NE + 1)
                    mm(banks[4][:, 0:CELLS], m_text, asum[:, :], start=True, stop=True)
                    mm(banks[4][:, CELLS:2 * CELLS], m_vis, asum[:, :], start=True, stop=True).then_inc(r_sum, 1)

                def down(e):
                    pe.wait_ge(f_alo, T * (NE * CH) + (e + 1) * CH)
                    for c in range(CELLS):
                        if e:
                            pe.wait_ge(f_yadd, T * (NE * CELLS) + (e - 1) * CELLS + c + 1)
                        at = lambda t, f: t[:, (e * CH + f) * D:(e * CH + f + 1) * D]
                        split_product(banks[4 + c][:, :], [
                            (a_hi[:, e % 2, f, c * P:(c + 1) * P], a_lo[:, e % 2, f, c * P:(c + 1) * P], at(w2_hi, f), at(w2_lo, f))
                            for f in range(CH)]).then_inc(g2_done, 1)

                pe.wait_ge(f_tlo, T * CELLS + CELLS)
                up(0)
                pe.wait_ge(r_top, T + 1)
                mm(banks[4][:, 0:2 * CELLS * NE], m_first, pick[:, :, :, :].rearrange("p k c e -> p (k c e)"),
                   start=True, stop=True).then_inc(r_pick, 1)
                up(1)
                pe.wait_ge(r_gate, T + 1)
                pe.wait_ge(w_lo_set, (2 * NIT + 1) * PIECES)
                down(0)
                up(2)
                down(1)
                turn_h(T + 1)
                pe.wait_ge(f_w_lo, FLATE)
                down(2)


_INS = ["x", "ctx_4096", "g_xattn", "g_ffn", "L0_xattn_Wq", "L0_xattn_Wk", "L0_xattn_Wv", "L0_xattn_Wo",
        "L0_xattn_q_norm_w", "L0_xattn_k_norm_w", "L0_ffn_gate_w", "L0_ffn_gate_b", "L0_ffn_w1", "L0_ffn_b1",
        "L0_ffn_w2", "L0_ffn_b2"]


def kernel(**inputs):
    import numpy as np
    import concourse.bacc as bacc
    from concourse.bass_utils import run_bass_kernel_spmd

    n = np.arange(P)
    same = n[:, None] // S == n[None, :] // S
    late = (n[:, None] % S >= VIS)
    consts = np.concatenate([np.eye(P), same & late, same & ~late, same & (n[:, None] % S == 0)], axis=1).astype(np.float32)

    nc = bacc.Bacc("TRN2", target_bir_lowering=False, num_devices=1)
    arrays, args = {}, []
    for name in _INS:
        a = np.ascontiguousarray(inputs[name])
        if name == "L0_ffn_b1":
            a = np.ascontiguousarray(a.reshape(NE * CH, P).T)
        arrays[f"in_{name}"] = a
        args.append(nc.dram_tensor(f"in_{name}", a.shape, mybir.dt.from_np(a.dtype), kind="ExternalInput").ap())
    arrays["consts"] = consts
    args.append(nc.dram_tensor("consts", consts.shape, mybir.dt.float32, kind="ExternalInput").ap())
    args.append(nc.dram_tensor("x2_scratch", (B * S, D), mybir.dt.float32, kind="Internal").ap())
    args.append(nc.dram_tensor("out", (B, S, D), mybir.dt.float32, kind="ExternalOutput").ap())
    flamingo_block(nc, *args)
    r = run_bass_kernel_spmd(nc, [arrays], core_ids=[0])
    return r.results[0]["out"]
```

```python
import concourse.bass as bass
from concourse import mybir
from contextlib import ExitStack

B, S, D = 32, 64, 512
HEADS, KVH, HD = 32, 8, 128
GRP = HEADS // KVH
NE = 3
P = 128
CH = D // P
NB = P // S
CELLS = 4
QUARTERS = B // (NB * CELLS)
ITS = KVH // 2
NIT = QUARTERS * ITS
STEPS = 2 * CELLS
NCELL = NIT * STEPS
PIECE = 512
PIECES = 10
RING = 5
WCOLS = PIECES * PIECE
SPLITS = [(0, 1, 2), (3, 4, 5), (6, 7), (8, 9)]
TILE = CH * NB * 2 * S
VIS = int(S * 0.3)
LN_EPS, RMS_EPS = 1e-5, 1e-6
FW = NE * CH * D
FPIECES = FW // PIECE
FEARLY = PIECES
FLATE = 2 * FPIECES - FEARLY
GT = P * CELLS
CHAIN = 23


def flamingo_block(nc, x, ctx_rows, g_xattn, g_ffn, wq, wk, wv, wo, qnw, knw, gate_w, gate_b, w1, b1, w2, b2, consts, x2_dram, out):
    fp32, f32r = mybir.dt.float32, mybir.dt.float32r
    ALU, ACT, AX = mybir.AluOpType, mybir.ActivationFunctionType, mybir.AxisListType

    x_rows = x.rearrange("b s d -> (b s) d").rearrange("(c p) d -> p c d", p=P)
    c_rows = ctx_rows.rearrange("b s d -> (b s) d").rearrange("(c p) d -> p c d", p=P)
    x2_rows = x2_dram.rearrange("(c p) d -> p c d", p=P)
    o_rows = out.rearrange("b s d -> (b s) d").rearrange("(c p) d -> p c d", p=P)
    wq_v = wq.rearrange("(c p) n -> p c n", p=P)
    wk_v = wk.rearrange("(c p) n -> p c n", p=P)
    wv_v = wv.rearrange("(c p) n -> p c n", p=P)
    wo_v = wo.rearrange("(h p) n -> p h n", p=P)
    w1_v = w1.rearrange("e (c p) n -> p (e c) n", p=P)
    w2_v = w2.rearrange("e (c p) n -> p (e c) n", p=P)

    es = ExitStack()
    with es:
        def sb(name, shape, dt=fp32):
            return es.enter_context(nc.sbuf_tensor(name, shape, dt))

        def sem(name):
            return es.enter_context(nc.semaphore(name))

        kvt_hi = sb("kvt_hi", [P, 2 * CELLS * TILE], f32r)
        kvt_lo = sb("kvt_lo", [P, 2 * CELLS * TILE], f32r)
        w_hi = sb("w_hi", [P, 2 * WCOLS], f32r)
        w_lo = sb("w_lo", [P, 2 * WCOLS], f32r)
        raw = sb("raw", [P, RING, PIECE])
        y = sb("y", [P, 2 * CELLS, D])
        rows3 = sb("rows3", [P, 3 * D])
        work = sb("work", [P, 26 * HD])
        at = [0]

        def part(k):
            at[0] += k * HD
            return work[:, at[0] - k * HD:at[0]]

        qhat = part(2 * GRP).rearrange("p (k g d) -> p k g d", k=2, g=GRP)
        khat = part(NB).rearrange("p (b d) -> p b d", b=NB)
        qT = part(GRP).rearrange("p (b g s) -> p b g s", b=NB, g=GRP)
        kT = part(NB).rearrange("p (b k) -> p b k", b=NB)
        prob = part(GRP).rearrange("p (r k) -> p r k", r=GRP)
        sq = part(GRP).rearrange("p (g d) -> p g d", g=GRP)
        first_xn = [rows3[:, 2 * D:], rows3[:, 0:D], rows3[:, D:2 * D], sq[:, :, :].rearrange("p g d -> p (g d)")]
        sqk = part(NB).rearrange("p (b d) -> p b d", b=NB)
        parts = sb("parts", [P, 6 * PIECE], f32r)
        v_hi, v_lo = (parts[:, i * PIECE:(i + 1) * PIECE].rearrange("p (k b d) -> p k b d", k=2, b=NB) for i in (0, 1))
        pT_hi, pT_lo = (parts[:, i * PIECE:(i + 1) * PIECE].rearrange("p (b r) -> p b r", b=NB) for i in (2, 3))
        oT_hi, oT_lo = (parts[:, i * PIECE:(i + 1) * PIECE].rearrange("p (g b s) -> p g b s", g=GRP, b=NB) for i in (4, 5))
        xrow, crow, xn = (rows3[:, i * D:(i + 1) * D] for i in range(3))
        gw_all = rows3[:, :]
        b2_all = work[:, 0:D * NE]
        act = work[:, D * NE:D * NE + 2 * GT].rearrange("p (k t) -> p k t", k=2)
        rjunk = work[:, D * NE + 2 * GT:D * NE + 2 * GT + D]
        cst = sb("cst", [P, 4 * P])
        ident, m_text, m_vis, m_first = (cst[:, i * P:(i + 1) * P] for i in range(4))
        ssq = sb("ssq", [P, 3, GRP])
        ssk = sb("ssk", [P, 3, NB])
        half = sb("half", [P, GRP])
        nmax = sb("nmax", [P, GRP])
        rsum = sb("rsum", [P, GRP])
        rinv = sb("rinv", [P, GRP])
        small = sb("small", [P, 8])
        bnst = sb("bnst", [P, CELLS, 6])
        mom = sb("mom", [P, 5, CELLS])
        mean = sb("mean", [P, CELLS])
        vare = sb("vare", [P, CELLS])
        rstd = sb("rstd", [P, CELLS])
        tanh_x, tanh_f, kw = small[:, 2:3], small[:, 3:4], small[:, 6:7]

        w1_hi, w1_lo = kvt_hi[:, 0:FW], kvt_lo[:, 0:FW]
        w2_hi, w2_lo = w_hi[:, 0:FW], w_lo[:, 0:FW]
        hT_hi, hT_lo = (t[:, FW:FW + CH * GT].rearrange("p (c t) -> p c t", c=CH) for t in (kvt_hi, kvt_lo))
        a_hi, a_lo = (t[:, FW:FW + 2 * CH * GT].rearrange("p (k f t) -> p k f t", k=2, f=CH) for t in (w_hi, w_lo))
        h = raw[:, 0:CELLS, :]
        b1_sb = sb("b1_sb", [P, NE * CH])
        asum = sb("asum", [P, CELLS])
        hg = sb("hg", [P, CELLS, NE])
        gwl = sb("gwl", [P, NE])
        gb = sb("gb", [P, NE])
        rt = sb("rt", [P, 20, CELLS])
        r3 = sb("r3", [P, 8, CELLS, NE])
        pick = sb("pick", [P, 2, CELLS, NE])
        gate = sb("gate", [P, CELLS, NE])
        b2_sb = b2_all.rearrange("p (e d) -> p e d", e=NE)
        gw_sb = gw_all.rearrange("p (d e) -> p d e", e=NE)

        banks = [es.enter_context(nc.psum_tensor(f"bank{i}", [P, 512], fp32)) for i in range(8)]
        ps_q, ps_kv, ps_tq, ps_tk, ps_s, ps_tp, ps_o, ps_y = banks

        s_cst, s_par, s_tanh, s_prod, s_kw, s_init = (sem(n) for n in ("consts_in", "params_in", "tanh_ready", "wprod", "kw_ready", "zeroed"))
        ld = [sem(f"raw_in{i}") for i in range(RING)]
        w_hi_set, w_lo_set = sem("w_hi_set"), sem("w_lo_set")
        xrow_in, crow_in, first_ctx = sem("xrow_in"), sem("crow_in"), sem("first_ctx_in")
        st_a, st_b, st_c, ln_pow, xn_set = (sem(n) for n in ("ln_stats", "ln_moments", "ln_eps", "ln_rstd", "xn_set"))
        lat_t, ctx_t, lat_hi, lat_lo, ctx_hi, ctx_lo = (sem(n) for n in ("lat_transposed", "ctx_transposed", "lat_hi_set", "lat_lo_set", "ctx_hi_set", "ctx_lo_set"))
        y_next = sem("y_next")
        x2_out = sem("x2_out")
        q_done, kv_done, tqk_done, s_done, tp_done, o_done, y_done = (sem(n) for n in (
            "q_done", "kv_done", "qk_transposed", "scores_done", "p_transposed", "o_done", "y_done"))
        q_sq, q_sum, q_eps, q_pow, q_set = (sem(n) for n in ("q_squared", "q_summed", "q_eps", "q_rsqrt", "qhat_set"))
        k_sq, k_eps, k_pow, k_set = (sem(n) for n in ("k_squared", "k_eps", "k_rsqrt", "khat_set"))
        vhi_set, vlo_set, qT_set, kT_set = (sem(n) for n in ("v_hi_set", "v_lo_set", "qT_set", "kT_set"))
        max_set, exp_set, inv_set, p_set = (sem(n) for n in ("max_set", "exp_set", "inv_set", "p_set"))
        pThi_set, pTlo_set, oThi_set, oTlo_set, y_added = (sem(n) for n in ("pT_hi_set", "pT_lo_set", "oT_hi_set", "oT_lo_set", "y_added"))

        f_x2, f_stats, f_mom, f_eps, f_pow, f_h, f_abs, f_out = (sem(n) for n in (
            "f_x2_in", "f_stats", "f_moments", "f_eps", "f_rstd", "f_h_set", "f_abs_set", "f_out"))
        f_t, f_thi, f_tlo, f_w_hi, f_bias = (sem(n) for n in (
            "f_transposed", "f_hT_hi", "f_hT_lo", "f_w_hi", "f_bias_in"))
        f_w_lo = (sem("f_w_lo_even"), sem("f_w_lo_odd"))
        g1_done, g2_done, f_act, f_ahi, f_alo, f_yadd = (sem(n) for n in (
            "up_done", "down_done", "act_set", "act_hi_set", "act_lo_set", "expert_added"))
        r_sum, r_lgt, r_exp, r_top, r_pick, r_gate, r_hg, chain = (sem(n) for n in (
            "router_sums", "router_logits", "router_exp", "router_top", "router_picked", "gates_set", "router_dots", "dve_chain"))

        def wait(eng, s, value):
            if not isinstance(value, int) or value > 0:
                eng.wait_ge(s, value)

        def slot_count(b, j):
            first, second = (32 if k in (4, 5) else 16 for k in (j % RING, j % RING + RING))
            return b * (first + second) + (first if j < RING else first + second)

        def w_piece(t, par, j):
            return t[:, par * WCOLS + j * PIECE:par * WCOLS + (j + 1) * PIECE]

        def wq_at(t, par, c):
            return w_piece(t, par, c)

        def wkv_at(t, par, c):
            return t[:, par * WCOLS + 2048 + c * 256:par * WCOLS + 2048 + (c + 1) * 256]

        def wo_at(t, par, h):
            return w_piece(t, par, 6 + h)

        def kvt_cell(t, par, cell):
            if isinstance(cell, int):
                v = t[:, (par * CELLS + cell) * TILE:(par * CELLS + cell + 1) * TILE]
            else:
                v = t[:, bass.ds(par * CELLS * TILE + cell * TILE, TILE)]
            return v.rearrange("p (c n) -> p c n", c=CH)

        def prep_dst(t, par, cell, src):
            v = kvt_cell(t, par, cell)
            if src == 1:
                return v[:, :, S:3 * S]
            return v.rearrange("p c (r s) -> p c r s", r=4)[:, :, 0:4:3, :]

        def late_piece(w1_part, w2_part, k):
            if k < FPIECES:
                return w1_part[:, k * PIECE:(k + 1) * PIECE]
            return w2_part[:, (FEARLY + k - FPIECES) * PIECE:(FEARLY + k - FPIECES + 1) * PIECE]

        def as_fp32(a):
            return a.bitcast(fp32)

        def bank_rows(b, src):
            v = b[:, :].rearrange("p (c t) -> p c t", c=CH)
            return v if src == 1 else v.rearrange("p c (b s) -> p c b s", b=NB)

        def first_bank(cell, src):
            return banks[(1 - src) * CELLS + cell]

        block = es.enter_context(nc.Block())

        @block.sync
        def _(sp):
            def load_piece(b, g, j):
                wait(sp, w_lo_set, b * PIECES + j - RING + 1 if not isinstance(b, int) or b * PIECES + j >= RING else 0)
                dst = raw[:, j % RING, :]
                if j < 4:
                    sp.dma_start(dst, wq_v[:, j, bass.ds(g * GRP * HD, PIECE)]).then_inc(ld[j % RING], 16)
                elif j < 6:
                    kv = dst.rearrange("p (c k n) -> p c k n", c=2, k=2)
                    c = 2 * (j - 4)
                    sp.dma_start(kv[:, :, 0, :], wk_v[:, c:c + 2, bass.ds(g * HD, HD)]).then_inc(ld[j % RING], 16)
                    sp.dma_start(kv[:, :, 1, :], wv_v[:, c:c + 2, bass.ds(g * HD, HD)]).then_inc(ld[j % RING], 16)
                else:
                    sp.dma_start(dst, wo_v[:, g * GRP + j - 6, :] if isinstance(g, int) else
                                 wo_v[:, bass.ds(g * GRP + j - 6, 1), :].rearrange("p a n -> p (a n)")).then_inc(ld[j % RING], 16)

            def load_rows(p, cell):
                wait(sp, xn_set, p)
                sp.dma_start(xrow[:, :], x_rows[:, bass.ds(cell, 1), :].rearrange("p a d -> p (a d)")).then_inc(xrow_in, 16)
                wait(sp, ctx_t, p)
                sp.dma_start(crow[:, :], c_rows[:, bass.ds(cell, 1), :].rearrange("p a d -> p (a d)")).then_inc(crow_in, 16)

            sp.dma_start(y[:, 0:CELLS, :], x_rows[:, 0:CELLS, :]).then_inc(y_next, 16)
            sp.dma_start(cst[:, :], consts).then_inc(s_cst, 16)
            for j in range(CELLS):
                load_piece(0, 0, j)
            sp.dma_start(y[:, CELLS:2 * CELLS, :], c_rows[:, 0:CELLS, :]).then_inc(first_ctx, 16)
            load_piece(0, 0, CELLS)
            for k, a in enumerate((g_xattn, g_ffn)):
                sp.dma_start(small[:, k:k + 1], a.partition_broadcast(P)).then_inc(s_par, 16)
            for k, a in enumerate((qnw, knw)):
                sp.dma_start(small[:, 4 + k:5 + k], a.rearrange("(p a) -> p a", a=1)).then_inc(s_par, 16)
            for j in range(RING, PIECES):
                load_piece(0, 0, j)
            for j in range(PIECES):
                load_piece(1, 1, j)
                if j == RING - 1:
                    sp.wait_ge(lat_t, CELLS)
                    load_rows(CELLS, CELLS)
            sp.wait_ge(y_added, 3)
            sp.dma_start(y[:, CELLS:2 * CELLS, :], x_rows[:, CELLS:2 * CELLS, :]).then_inc(y_next, 16)

            def iteration_loads(q, gp):
                it = q * ITS + gp
                wrap = isinstance(gp, int) and gp == ITS - 1
                for j in range(PIECES):
                    load_piece(it * 2 + 2, 0 if wrap else gp * 2 + 2, j)
                for j in range(PIECES):
                    load_piece(it * 2 + 3, 1 if wrap else gp * 2 + 3, j)
                cell = it + CELLS + 1
                load_rows(cell, sp.snap(cell % (CELLS * QUARTERS)))

            iteration_loads(0, 0)
            def quarter_loads(q):
                with sp.Fori(1, ITS - 1) as gp:
                    iteration_loads(q, gp)
                iteration_loads(q, ITS - 1)
                iteration_loads(q + 1, 0)

            with sp.Fori(0, QUARTERS - 2) as q:
                quarter_loads(q)
                done = y[:, bass.ds(sp.snap((q % 2) * CELLS), CELLS), :]
                coming = sp.snap((q + 2) * CELLS)
                sp.wait_ge(y_added, (q + 1) * (STEPS * ITS) + 3)
                sp.dma_start(x2_rows[:, bass.ds(q * CELLS, CELLS), :], done).then_inc(x2_out, 16)
                sp.wait_ge(x2_out, (q + 1) * 16)
                sp.dma_start(done, x_rows[:, bass.ds(coming, CELLS), :]).then_inc(y_next, 16)
            quarter_loads(QUARTERS - 2)
            with sp.Fori(1, ITS - 1) as gp:
                iteration_loads(QUARTERS - 1, gp)

            for j in range(FEARLY):
                sp.wait_ge(w_lo_set, 2 * NIT * PIECES + j - RING + 1)
                halves = 2 if j in (4, 5) else 1
                for k in range(halves):
                    cols = slice(k * PIECE // halves, (k + 1) * PIECE // halves)
                    sp.dma_start(raw[:, j % RING, cols], w2_v[:, j, cols]).then_inc(ld[j % RING], 16)
            for k in range(FLATE):
                if k < RING:
                    sp.wait_ge(w_lo_set, (2 * NIT + 1) * PIECES + k - RING + 1)
                else:
                    sp.wait_ge(f_w_lo[(k - RING) % 2], (k - RING) // 2 + 1)
                sp.dma_start(raw[:, k % RING, :], w1_v[:, k, :] if k < FPIECES else w2_v[:, FEARLY + k - FPIECES, :]).then_inc(ld[k % RING], 16)
                if k == RING - 1:
                    sp.wait_ge(ctx_t, NIT + CELLS)
                    sp.dma_start(gw_all, gate_w[0:D, :].rearrange("d e -> (d e)").partition_broadcast(P)).then_inc(f_bias, 16)
                    sp.dma_start(gwl[:, :], gate_w[D:D + 1, :].rearrange("d e -> (d e)").partition_broadcast(P)).then_inc(f_bias, 16)
                    sp.dma_start(gb[:, :], gate_b.partition_broadcast(P)).then_inc(f_bias, 16)
                    sp.dma_start(b1_sb[:, :], b1).then_inc(f_bias, 16)
            sp.wait_ge(s_done, NCELL + 1)
            sp.dma_start(b2_all, b2.rearrange("e d -> (e d)").partition_broadcast(P)).then_inc(f_bias, 16)
            sp.wait_ge(y_next, QUARTERS * 16)
            for T in range(QUARTERS):
                half_y = y[:, T % 2 * CELLS:(T % 2 + 1) * CELLS, :]
                out_c = (T + 2) % QUARTERS * CELLS
                for c in range(CELLS):
                    sp.wait_ge(f_yadd, T * NE * CELLS + (NE - 1) * CELLS + c + 1)
                    sp.dma_start(o_rows[:, out_c + c, :], half_y[:, c, :]).then_inc(f_out, 16)
                if T + 2 < QUARTERS:
                    sp.wait_ge(f_out, (T + 1) * CELLS * 16)
                    sp.dma_start(half_y, x2_rows[:, T * CELLS:(T + 1) * CELLS, :]).then_inc(f_x2, 16)
            sp.wait_ge(f_out, QUARTERS * CELLS * 16)

        @block.gpsimd
        def _(pool):
            pow_ = lambda out, a, n: nc.gpsimd.tensor_tensor(out, a, half[:, 0:n], ALU.pow)

            def low_piece(b, j, par):
                pool.wait_ge(w_hi_set, b * PIECES + j + 1)
                nc.gpsimd.tensor_tensor(w_piece(w_lo, par, j), raw[:, j % RING, :], as_fp32(w_piece(w_hi, par, j)),
                                        ALU.subtract).then_inc(w_lo_set, 1)

            def ln_power(n, count):
                pool.wait_ge(st_c, count + 1)
                pow_(rstd[:, 0:n], vare[:, 0:n], n).then_inc(ln_pow, 1)

            nc.gpsimd.memset(as_fp32(w_hi[:, WCOLS + 6 * PIECE:2 * WCOLS]), 0.0)
            nc.gpsimd.memset(as_fp32(w_lo[:, WCOLS + 6 * PIECE:2 * WCOLS]), 0.0).then_inc(y_added, 1)
            pool.wait_ge(s_init, 1)
            ln_power(CELLS, 0)
            for j in range(PIECES):
                low_piece(0, j, 0)
            with pool.Fori(0, NIT) as it:
                for s in range(STEPS):
                    i = it * STEPS + s
                    pool.wait_ge(q_eps, i + 1)
                    pow_(ssq[:, 2, :], ssq[:, 1, :], GRP).then_inc(q_pow, 1)
                    for j in SPLITS[s % CELLS]:
                        low_piece(it * 2 + s // CELLS + 1, j, 1 - s // CELLS)
                    pool.wait_ge(k_eps, i + 1)
                    pow_(ssk[:, 2, :], ssk[:, 1, :], NB).then_inc(k_pow, 1)
                    if s == 3:
                        ln_power(1, it + 1)
            def ffn_power(T):
                pool.wait_ge(f_eps, T + 1)
                pow_(rstd[:, :], vare[:, :], CELLS).then_inc(f_pow, 1)

            for k in range(0, FLATE, 2):
                pool.wait_ge(f_w_hi, k + 1)
                nc.gpsimd.tensor_tensor(late_piece(w1_lo, w2_lo, k), raw[:, k % RING, :], as_fp32(late_piece(w1_hi, w2_hi, k)),
                                        ALU.subtract).then_inc(f_w_lo[0], 1)
                if k == 8:
                    ffn_power(0)
            with pool.Fori(1, QUARTERS + 1) as T:
                ffn_power(T)

        @block.scalar
        def _(act_e):
            def high_piece(b, j, par):
                act_e.wait_ge(ld[j % RING], slot_count(b, j))
                nc.scalar.activation(w_piece(w_hi, par, j), raw[:, j % RING, :], ACT.Copy).then_inc(w_hi_set, 1)

            def q_part(i):
                act_e.wait_ge(q_done, i + 1)
                nc.scalar.activation(sq[:, :, :].rearrange("p g d -> p (g d)"), ps_q[:, :], ACT.Square).then_inc(q_sq, 1)

            def p_high(m):
                act_e.wait_ge(tp_done, m + 3)
                nc.scalar.activation(pT_hi[:, :, :].rearrange("p b r -> p (b r)"), ps_tp[:, :], ACT.Copy).then_inc(pThi_set, 1)

            def o_high(m):
                act_e.wait_ge(o_done, m + 3)
                nc.scalar.activation(oT_hi[:, :, :, :], ps_o[:, :].rearrange("p (b g s) -> p g b s", b=NB, g=GRP),
                                     ACT.Copy).then_inc(oThi_set, 1)

            def q_turned(m):
                act_e.wait_ge(tqk_done, m + 2)
                nc.scalar.activation(qT[:, :, :, :], ps_tq[:, :].rearrange("p (g b s) -> p b g s", g=GRP, b=NB),
                                     ACT.Copy).then_inc(qT_set, 1)

            def kv_part(i, s):
                act_e.wait_ge(kv_done, i + 1)
                kv = ps_kv[:, :].rearrange("p (b k d) -> p b k d", b=NB, k=2)
                for b in range(NB):
                    last = nc.scalar.activation(sqk[:, b, :], kv[:, b, 0, :], ACT.Square, accum_out=ssk[:, 0, b:b + 1])
                last.then_inc(k_sq, 1)
                nc.scalar.activation(v_hi[:, s % 2, :, :], kv[:, :, 1, :], ACT.Copy, scale=tanh_x).then_inc(vhi_set, 1)

            def softmax(m):
                act_e.wait_ge(max_set, m + 2)
                for r in range(GRP):
                    last = nc.scalar.activation(prob[:, r, :], ps_s[:, r * HD:(r + 1) * HD], ACT.Exp,
                                                bias=nmax[:, r:r + 1], accum_out=rsum[:, r:r + 1])
                last.then_inc(exp_set, 1)

            def first_turned(cell, src):
                turned, hi_set = ((ctx_t, ctx_hi), (lat_t, lat_hi))[src]
                act_e.wait_ge(turned, cell + 1)
                nc.scalar.activation(prep_dst(kvt_hi, 0, cell, src), bank_rows(first_bank(cell, src), src), ACT.Copy).then_inc(hi_set, 1)

            for j in range(CELLS):
                high_piece(0, j, 0)
            for src in (1, 0):
                for c in range(CELLS):
                    first_turned(c, src)
            act_e.wait_ge(s_par, 64)
            nc.scalar.activation(small[:, 2:4], small[:, 0:2], ACT.Tanh).then_inc(s_tanh, 1)
            for j in range(CELLS, PIECES):
                high_piece(0, j, 0)
            act_e.wait_ge(s_tanh, 1)
            with act_e.Fori(0, NIT) as it:
                for s in range(STEPS):
                    i = it * STEPS + s
                    p_high(i - 2)
                    q_part(i)
                    if s % CELLS == 2:
                        act_e.wait_ge(y_done, i)
                    for j in SPLITS[s % CELLS]:
                        high_piece(it * 2 + s // CELLS + 1, j, 1 - s // CELLS)
                    o_high(i - 2)
                    q_turned(i - 1)
                    kv_part(i, s)
                    softmax(i - 1)
            def late_high(k):
                act_e.wait_ge(ld[k % RING], slot_count(2 * NIT, PIECES - RING + k % RING) + 16 * (k // RING + 1))
                nc.scalar.activation(late_piece(w1_hi, w2_hi, k), raw[:, k % RING, :], ACT.Copy).then_inc(f_w_hi, 1)

            act_e.wait_ge(ctx_lo, NIT + CELLS)
            q_turned(NCELL - 1)
            late_high(0)
            p_high(NCELL - 2)
            late_high(1)
            late_high(2)
            o_high(NCELL - 2)
            softmax(NCELL - 1)
            for k in range(3, 6):
                late_high(k)
            p_high(NCELL - 1)
            late_high(6)
            late_high(7)
            o_high(NCELL - 1)
            for k in range(8, FLATE):
                late_high(k)

            def turned_high(T):
                for c in range(CELLS):
                    act_e.wait_ge(f_t, T * CELLS + c + 1)
                    nc.scalar.activation(hT_hi[:, :, c * P:(c + 1) * P], banks[c][:, :].rearrange("p (c t) -> p c t", c=CH),
                                         ACT.Copy).then_inc(f_thi, 1)

            def strengths(T):
                for c in range(CELLS):
                    last = nc.scalar.activation(act[:, c % 2, :], h[:, c, :], ACT.Abs, accum_out=asum[:, c:c + 1])
                    if c % 2:
                        last.then_inc(f_abs, 1)
                        act_e.wait_ge(f_abs, T * 2 + c // 2 + 1)

            turned_high(0)
            strengths(0)
            act_e.wait_ge(f_bias, 80)
            with act_e.Fori(0, QUARTERS) as T:
                act_e.wait_ge(r_lgt, T + 1)
                nc.scalar.activation(r3[:, 2, :, :], r3[:, 1, :, :], ACT.Exp).then_inc(r_exp, 1)
                for e, func in enumerate((ACT.Tanh, ACT.Gelu, ACT.Silu)):
                    for f in range(CH):
                        k = T * (NE * CH) + e * CH + f
                        act_e.wait_ge(g1_done, k + 1)
                        if e or f >= 2:
                            act_e.wait_ge(f_alo, k - 1)
                        nc.scalar.activation(act[:, f % 2, :], banks[f][:, :], func,
                                             bias=b1_sb[:, e * CH + f:e * CH + f + 1]).then_inc(f_act, 1)
                turned_high(T + 1)
                act_e.wait_ge(f_alo, T * (NE * CH) + NE * CH)
                strengths(T + 1)

        @block.vector
        def _(dve):
            V = nc.vector

            def moments(n, summed, squared, done, count):
                stat = bnst[:, 0:n, :].rearrange("p c (k t) -> p c k t", k=2)
                dve.wait_ge(summed, count + 1)
                V.tensor_tensor(mom[:, 0, 0:n], stat[:, :, 0, 1], stat[:, :, 1, 1], ALU.add)
                V.tensor_tensor(mom[:, 1, 0:n], stat[:, :, 0, 1], stat[:, :, 1, 1], ALU.subtract)
                V.tensor_tensor(mom[:, 2, 0:n], stat[:, :, 0, 2], stat[:, :, 1, 2], ALU.add).then_inc(squared, 1)
                dve.wait_ge(squared, 2 * count + 1)
                V.tensor_scalar(mean[:, 0:n], mom[:, 0, 0:n], 0.5, None, ALU.mult)
                V.tensor_scalar(mom[:, 3, 0:n], mom[:, 2, 0:n], 1.0 / D, LN_EPS, ALU.mult, ALU.add)
                V.tensor_tensor(mom[:, 4, 0:n], mom[:, 1, 0:n], mom[:, 1, 0:n], ALU.mult).then_inc(squared, 1)
                dve.wait_ge(squared, 2 * count + 2)
                V.scalar_tensor_tensor(vare[:, 0:n], mom[:, 4, 0:n], 0.25, mom[:, 3, 0:n], ALU.mult, ALU.add).then_inc(done, 1)

            def ln_stats(it):
                dve.wait_ge(xrow_in, it * 16 + 16)
                V.bn_stats(bnst[:, 0, :], xrow).then_inc(st_a, 1)
                moments(1, st_a, st_b, st_c, it + 1)

            def ln_apply(it):
                dve.wait_ge(ln_pow, it + 2)
                V.tensor_scalar(xn, xrow, mean[:, 0:1], rstd[:, 0:1], ALU.subtract, ALU.mult).then_inc(xn_set, 1)

            def first_low(cell, src):
                hi_set, lo_set = ((ctx_hi, ctx_lo), (lat_hi, lat_lo))[src]
                dve.wait_ge(hi_set, cell + 1)
                V.tensor_tensor(prep_dst(kvt_lo, 0, cell, src), bank_rows(first_bank(cell, src), src),
                                as_fp32(prep_dst(kvt_hi, 0, cell, src)), ALU.subtract).then_inc(lo_set, 1)

            def rows_turned(p, par, cell, src):
                turned, hi_set, lo_set = ((ctx_t, ctx_hi, ctx_lo), (lat_t, lat_hi, lat_lo))[src]
                dst_hi, dst_lo = prep_dst(kvt_hi, par, cell, src), prep_dst(kvt_lo, par, cell, src)
                dve.wait_ge(turned, p + 1)
                V.tensor_scalar(dst_hi, bank_rows(ps_tq, src), 1.0, None, ALU.mult).then_inc(hi_set, 1)
                dve.wait_ge(hi_set, p + 1)
                V.tensor_tensor(dst_lo, bank_rows(ps_tq, src), as_fp32(dst_hi), ALU.subtract).then_inc(lo_set, 1)

            def scale_q(i, s):
                dve.wait_ge(q_pow, i + 1)
                V.tensor_tensor(qhat[:, s % 2, :, :], ps_q[:, :].rearrange("p (g d) -> p g d", g=GRP),
                                ssq[:, 2, :].unsqueeze(2).to_broadcast([P, GRP, HD]), ALU.mult).then_inc(q_set, 1)

            def sum_q(i):
                dve.wait_ge(q_sq, i + 1)
                V.tensor_reduce(ssq[:, 0, :], sq[:, :, :], AX.X, ALU.add).then_inc(q_sum, 1)
                dve.wait_ge(q_sum, i + 1)
                V.tensor_scalar(ssq[:, 1, :], ssq[:, 0, :], RMS_EPS * HD, None, ALU.add).then_inc(q_eps, 1)

            def p_low(m):
                dve.wait_ge(pThi_set, m + 3)
                V.tensor_tensor(pT_lo[:, :, :].rearrange("p b r -> p (b r)"), ps_tp[:, :],
                                as_fp32(pT_hi[:, :, :]).rearrange("p b r -> p (b r)"), ALU.subtract).then_inc(pTlo_set, 1)

            def o_low(m):
                dve.wait_ge(oThi_set, m + 3)
                V.tensor_tensor(oT_lo[:, :, :, :], ps_o[:, :].rearrange("p (b g s) -> p g b s", b=NB, g=GRP),
                                as_fp32(oT_hi[:, :, :, :]), ALU.subtract).then_inc(oTlo_set, 1)

            def k_turned(m):
                dve.wait_ge(tqk_done, m + 2)
                V.tensor_scalar(kT[:, :, :].rearrange("p b k -> p (b k)"), ps_tk[:, 0:NB * HD], kw, None, ALU.mult).then_inc(kT_set, 1)

            def k_sum_v_low(i, s):
                dve.wait_ge(k_sq, i + 1)
                V.tensor_scalar(ssk[:, 1, :], ssk[:, 0, :], RMS_EPS * HD, None, ALU.add).then_inc(k_eps, 1)
                kv = ps_kv[:, :].rearrange("p (b k d) -> p b k d", b=NB, k=2)
                dve.wait_ge(vhi_set, i + 1)
                V.scalar_tensor_tensor(v_lo[:, s % 2, :, :], kv[:, :, 1, :], tanh_x, as_fp32(v_hi[:, s % 2, :, :]),
                                       ALU.mult, ALU.subtract).then_inc(vlo_set, 1)

            def row_max(m):
                dve.wait_ge(s_done, m + 2)
                V.tensor_reduce(nmax[:, :], ps_s[:, :].rearrange("p (r k) -> p r k", r=GRP), AX.X, ALU.max,
                                negate=True).then_inc(max_set, 1)

            def scale_k(i):
                dve.wait_ge(k_pow, i + 1)
                kv = ps_kv[:, :].rearrange("p (b k d) -> p b k d", b=NB, k=2)
                V.tensor_tensor(khat[:, :, :], kv[:, :, 0, :], ssk[:, 2, :].unsqueeze(2).to_broadcast([P, NB, HD]),
                                ALU.mult).then_inc(k_set, 1)

            def normalise(m):
                dve.wait_ge(exp_set, m + 2)
                V.reciprocal(rinv[:, :], rsum[:, :]).then_inc(inv_set, 1)
                dve.wait_ge(inv_set, m + 2)
                V.tensor_tensor(prob[:, :, :], prob[:, :, :], rinv[:, :].unsqueeze(2).to_broadcast([P, GRP, HD]),
                                ALU.mult).then_inc(p_set, 1)

            def add_y(m, c):
                dve.wait_ge(y_done, m + 3)
                slot = (m + 2 * STEPS * ITS) // (STEPS * ITS) % 2 * CELLS + c
                yt = y[:, slot, :] if isinstance(slot, int) else y[:, bass.ds(slot, 1), :].rearrange("p a d -> p (a d)")
                V.tensor_tensor(yt, ps_y[:, :], yt, ALU.add).then_inc(y_added, 1)

            V.memset(as_fp32(v_hi[:, :, :, :]).rearrange("p k b d -> p (k b d)"), 0.0)
            V.memset(as_fp32(v_lo[:, :, :, :]).rearrange("p k b d -> p (k b d)"), 0.0).then_inc(vlo_set, 1)
            V.memset(qhat[:, 1, :, :].rearrange("p g d -> p (g d)"), 0.0).then_inc(q_set, 1)
            V.memset(khat[:, :, :].rearrange("p b d -> p (b d)"), 0.0).then_inc(k_set, 1)
            V.memset(prob[:, :, :].rearrange("p g d -> p (g d)"), 0.0).then_inc(p_set, 1)
            V.memset(hg[:, :, :], 0.0).then_inc(f_x2, 1)
            V.memset(half[:, :], -0.5).then_inc(s_init, 1)
            dve.wait_ge(y_next, 16)
            for c in range(CELLS):
                last = V.bn_stats(bnst[:, c, :], y[:, c, :])
            last.then_inc(st_a, 1)
            moments(CELLS, st_a, st_b, st_c, 0)
            dve.wait_ge(ln_pow, 1)
            for c in range(CELLS):
                V.tensor_scalar(first_xn[c], y[:, c, :], mean[:, c:c + 1], rstd[:, c:c + 1], ALU.subtract, ALU.mult).then_inc(xn_set, 1)
            for src in (1, 0):
                for c in range(CELLS):
                    first_low(c, src)
            dve.wait_ge(s_par, 64)
            V.tensor_tensor(small[:, 7:8], small[:, 4:5], small[:, 5:6], ALU.mult).then_inc(s_prod, 1)
            dve.wait_ge(s_prod, 1)
            V.tensor_scalar(kw, small[:, 7:8], float(HD) ** 0.5, None, ALU.mult).then_inc(s_kw, 1)
            dve.wait_ge(s_kw, 1)
            dve.wait_ge(s_tanh, 1)
            with dve.Fori(0, NIT) as it:
                for s in range(STEPS):
                    i = it * STEPS + s
                    p = it + CELLS
                    p_low(i - 2)
                    sum_q(i)
                    k_turned(i - 1)
                    scale_q(i, s)
                    o_low(i - 2)
                    k_sum_v_low(i, s)
                    row_max(i - 1)
                    scale_k(i)
                    normalise(i - 1)
                    if s in (5, 6):
                        rows_turned(p, 0, (it // ITS + 1) % 2 * CELLS + it % ITS, 6 - s)
                    if s == 0:
                        dve.wait_ge(y_next, it // ITS * 16 + 16)
                    add_y(i - 2, (s - 2) % CELLS)
                    if s == 3:
                        ln_stats(it)
                    if s == 4:
                        ln_apply(it)
            def ffn_stats(rows, cells):
                for c in cells:
                    last = V.bn_stats(bnst[:, c, :], rows[:, c, :])
                return last

            def ffn_normalise(T, rows):
                dve.wait_ge(f_pow, T + 1)
                for c in range(CELLS):
                    V.tensor_scalar(h[:, c, :], rows[:, c, :], mean[:, c:c + 1], rstd[:, c:c + 1], ALU.subtract, ALU.mult).then_inc(f_h, 1)

            def turned_low(T):
                for c in range(CELLS):
                    dve.wait_ge(f_thi, T * CELLS + c + 1)
                    V.tensor_tensor(hT_lo[:, :, c * P:(c + 1) * P], banks[c][:, :].rearrange("p (c t) -> p c t", c=CH),
                                    as_fp32(hT_hi[:, :, c * P:(c + 1) * P]), ALU.subtract).then_inc(f_tlo, 1)

            def router_dots(T, c):
                for e in range(NE):
                    V.tensor_tensor_reduce(out=rjunk, in0=h[:, c, :], in1=gw_sb[:, :, e], scale=1.0, scalar=0.0,
                                           op0=ALU.mult, op1=ALU.add, accum_out=hg[:, c, e:e + 1]).then_inc(r_hg, 1)
                    dve.wait_ge(r_hg, T * (CELLS * NE) + c * NE + e + 1)

            halves = [y[:, par * CELLS:(par + 1) * CELLS, :] for par in range(2)]
            def late_low(k):
                dve.wait_ge(f_w_hi, k + 1)
                V.tensor_tensor(late_piece(w1_lo, w2_lo, k), raw[:, k % RING, :], as_fp32(late_piece(w1_hi, w2_hi, k)),
                                ALU.subtract).then_inc(f_w_lo[1], 1)

            k_turned(NCELL - 1)
            p_low(NCELL - 2)
            row_max(NCELL - 1)
            late_low(1)
            o_low(NCELL - 2)
            ffn_stats(halves[0], (0, 1))
            normalise(NCELL - 1)
            ffn_stats(halves[0], (2, 3)).then_inc(f_stats, 1)
            late_low(3)
            p_low(NCELL - 1)
            moments(CELLS, f_stats, f_mom, f_eps, 0)
            add_y(NCELL - 2, CELLS - 2)
            late_low(5)
            o_low(NCELL - 1)
            for k in range(7, FLATE, 2):
                late_low(k)
            for k in range(2):
                dve.wait_ge(f_w_lo[k], FLATE // 2)
            ffn_normalise(0, halves[0])
            add_y(NCELL - 1, CELLS - 1)

            turned_low(0)
            dve.wait_ge(f_bias, 80)
            for c in range(CELLS):
                router_dots(0, c)

            def ffn_group(j, par):
                T = j * 2 + par
                mine, coming = halves[par], halves[1 - par]
                links = [0]

                def link(ins):
                    links[0] += 1
                    ins.then_inc(chain, 1)
                    dve.wait_ge(chain, T * CHAIN + links[0])

                def split_act(e, f):
                    k = T * (NE * CH) + e * CH + f
                    dve.wait_ge(f_act, k + 1)
                    V.tensor_copy(a_hi[:, e % 2, f, :], act[:, f % 2, :]).then_inc(f_ahi, 1)
                    dve.wait_ge(f_ahi, k + 1)
                    V.tensor_tensor(a_lo[:, e % 2, f, :], act[:, f % 2, :], as_fp32(a_hi[:, e % 2, f, :]),
                                    ALU.subtract).then_inc(f_alo, 1)

                def add_expert(e, c):
                    n = T * (NE * CELLS) + e * CELLS + c
                    dve.wait_ge(g2_done, n + 1)
                    if e:
                        dve.wait_ge(f_yadd, n - CELLS + 1)
                    V.scalar_tensor_tensor(mine[:, c, :], banks[4 + c][:, :], gate[:, c, e:e + 1], mine[:, c, :],
                                           ALU.mult, ALU.add).then_inc(f_yadd, 1)

                bc = lambda a: a.unsqueeze(2).to_broadcast([P, CELLS, NE])
                be = lambda a: a.unsqueeze(1).to_broadcast([P, CELLS, NE])
                dve.wait_ge(r_sum, T + 1)
                V.tensor_scalar(rt[:, 0, :], banks[4][:, 0:CELLS], 1.0 / ((S - VIS) * D), None, ALU.mult)
                link(V.tensor_scalar(rt[:, 1, :], banks[4][:, CELLS:2 * CELLS], 1.0 / (VIS * D), 1e-8, ALU.mult, ALU.add))
                link(V.reciprocal(rt[:, 2, :], rt[:, 1, :]))
                link(V.tensor_tensor(rt[:, 3, :], rt[:, 0, :], rt[:, 2, :], ALU.mult))
                link(V.tensor_tensor(r3[:, 0, :, :], bc(rt[:, 3, :]), be(gwl[:, :]), ALU.mult))
                link(V.tensor_tensor(r3[:, 3, :, :], r3[:, 0, :, :], hg[:, :, :], ALU.add))
                link(V.tensor_tensor(r3[:, 4, :, :], r3[:, 3, :, :], be(gb[:, :]), ALU.add))
                link(V.tensor_reduce(rt[:, 4, :], r3[:, 4, :, :], AX.X, ALU.max))
                V.tensor_tensor(r3[:, 1, :, :], r3[:, 4, :, :], bc(rt[:, 4, :]), ALU.subtract).then_inc(r_lgt, 1)
                dve.wait_ge(r_exp, T + 1)
                link(V.tensor_reduce(rt[:, 5, :], r3[:, 2, :, :], AX.X, ALU.add))
                link(V.reciprocal(rt[:, 6, :], rt[:, 5, :]))
                score = r3[:, 5, :, :]
                link(V.tensor_tensor(score, r3[:, 2, :, :], bc(rt[:, 6, :]), ALU.mult))
                s0, s1, s2 = (r3[:, 5, :, e] for e in range(NE))
                c01, c02, c12 = rt[:, 7, :], rt[:, 8, :], rt[:, 9, :]
                V.tensor_tensor(c01, s0, s1, ALU.is_ge)
                V.tensor_tensor(c02, s0, s2, ALU.is_ge)
                link(V.tensor_tensor(c12, s1, s2, ALU.is_ge))
                rank = r3[:, 6, :, :]
                V.tensor_tensor(rt[:, 10, :], c01, c02, ALU.add)
                V.tensor_tensor(rt[:, 11, :], c01, c12, ALU.subtract)
                link(V.tensor_tensor(r3[:, 6, :, 2], c02, c12, ALU.add))
                V.tensor_scalar(r3[:, 6, :, 0], rt[:, 10, :], -1.0, 2.0, ALU.mult, ALU.add)
                link(V.tensor_scalar(r3[:, 6, :, 1], rt[:, 11, :], 1.0, None, ALU.add))
                V.tensor_scalar(pick[:, 0, :, :], rank, 0.0, None, ALU.is_equal)
                V.tensor_scalar(pick[:, 1, :, :], rank, 1.0, None, ALU.is_equal).then_inc(r_top, 1)
                dve.wait_ge(r_top, T + 1)
                V.tensor_reduce(rt[:, 12, :], score, AX.X, ALU.max)
                link(V.tensor_tensor(r3[:, 7, :, :], score, pick[:, 1, :, :], ALU.mult))
                link(V.tensor_reduce(rt[:, 13, :], r3[:, 7, :, :], AX.X, ALU.add))
                link(V.scalar_tensor_tensor(rt[:, 14, :], rt[:, 12, :], 1e-8, rt[:, 13, :], ALU.add, ALU.add))
                link(V.reciprocal(rt[:, 15, :], rt[:, 14, :]))
                link(V.tensor_scalar(rt[:, 16, :], rt[:, 15, :], tanh_f, None, ALU.mult))
                V.tensor_tensor(rt[:, 17, :], rt[:, 12, :], rt[:, 16, :], ALU.mult)
                link(V.tensor_tensor(rt[:, 18, :], rt[:, 13, :], rt[:, 16, :], ALU.mult))

                for f in range(CH):
                    split_act(0, f)
                dve.wait_ge(r_pick, T + 1)
                picked = banks[4][:, 0:2 * CELLS * NE].rearrange("p (k c e) -> p k c e", k=2, c=CELLS)
                V.tensor_tensor(r3[:, 0, :, :], picked[:, 0, :, :], bc(rt[:, 17, :]), ALU.mult)
                link(V.tensor_tensor(r3[:, 3, :, :], picked[:, 1, :, :], bc(rt[:, 18, :]), ALU.mult))
                V.tensor_tensor(gate[:, :, :], r3[:, 0, :, :], r3[:, 3, :, :], ALU.add).then_inc(r_gate, 1)
                dve.wait_ge(r_gate, T + 1)
                for e in range(NE):
                    for c in range(CELLS):
                        last = V.scalar_tensor_tensor(mine[:, c, :], b2_sb[:, e, :], gate[:, c, e:e + 1], mine[:, c, :], ALU.mult, ALU.add)
                    link(last)
                for f in range(CH):
                    split_act(1, f)
                for c in range(CELLS):
                    add_expert(0, c)
                dve.wait_ge(f_x2, 17 if par else j * 32 + 1)
                ffn_stats(coming, range(CELLS)).then_inc(f_stats, 1)
                moments(CELLS, f_stats, f_mom, f_eps, T + 1)
                dve.wait_ge(f_abs, T * 2 + 2)
                ffn_normalise(T + 1, coming)
                for f in range(CH):
                    split_act(2, f)
                for c in range(CELLS):
                    add_expert(1, c)
                turned_low(T + 1)
                for c in range(CELLS):
                    router_dots(T + 1, c)
                    add_expert(2, c)
                assert links[0] == CHAIN, links

            with dve.Fori(0, QUARTERS // 2) as j:
                for par in range(2):
                    ffn_group(j, par)

        @block.tensor
        def _(pe):
            mm = nc.tensor.matmul

            def split_product(out, pairs, before_last=None):
                n = len(pairs)
                for k, (a_hi_, a_lo_, b_hi_, b_lo_) in enumerate(pairs):
                    if before_last is not None and k == n - 1:
                        before_last()
                    mm(out, a_hi_, b_hi_, start=k == 0, stop=False)
                    mm(out, a_hi_, b_lo_, start=False, stop=False)
                    last = mm(out, a_lo_, b_hi_, start=False, stop=k == n - 1)
                return last

            def turn_into(bank, rows, done):
                for c in range(CH):
                    last = nc.tensor.transpose(bank[:, c * P:(c + 1) * P], rows[:, c * P:(c + 1) * P], ident)
                last.then_inc(done, 1)

            def turn(it, src):
                if src == 1:
                    pe.wait_ge(xn_set, it + CELLS + 1)
                    turn_into(ps_tq, xn, lat_t)
                else:
                    pe.wait_ge(crow_in, it * 16 + 16)
                    turn_into(ps_tq, crow, ctx_t)

            def project_q(m, kpar, cell, wpar):
                hi, lo = kvt_cell(kvt_hi, kpar, cell), kvt_cell(kvt_lo, kpar, cell)
                return split_product(ps_q[:, :], [(hi[:, c, S:3 * S], lo[:, c, S:3 * S], wq_at(w_hi, wpar, c), wq_at(w_lo, wpar, c))
                                                  for c in range(CH)], before_last=lambda: turn_p(m))

            def project_kv(b, kpar, cell, wpar):
                hi, lo = kvt_cell(kvt_hi, kpar, cell), kvt_cell(kvt_lo, kpar, cell)
                rows = lambda t, c: t[:, c, b * 2 * S:(b + 1) * 2 * S]
                return split_product(ps_kv[:, b * 2 * HD:(b + 1) * 2 * HD], [
                    (rows(hi, c), rows(lo, c), wkv_at(w_hi, wpar, c), wkv_at(w_lo, wpar, c)) for c in range(CH)])

            def turn_p(m):
                pe.wait_ge(p_set, m + 3)
                for r in range(GRP):
                    last = nc.tensor.transpose(ps_tp[:, r * P:(r + 1) * P], prob[:, r, :], ident)
                last.then_inc(tp_done, 1)

            def weigh_v(m, s):
                pe.wait_ge(pTlo_set, m + 3)
                for b in range(NB):
                    k = s % 2
                    last = split_product(ps_o[:, b * GRP * S:(b + 1) * GRP * S], [
                        (v_hi[:, k, b, :], v_lo[:, k, b, :], pT_hi[:, b, :], pT_lo[:, b, :])])
                last.then_inc(o_done, 1)

            def turn_qk(m, s):
                for g in range(GRP):
                    nc.tensor.transpose(ps_tq[:, g * P:(g + 1) * P], qhat[:, s % 2, g, :], ident)
                for b in range(NB):
                    last = nc.tensor.transpose(ps_tk[:, b * P:(b + 1) * P], khat[:, b, :], ident)
                last.then_inc(tqk_done, 1)

            def scores(m):
                pe.wait_ge(qT_set, m + 2)
                pe.wait_ge(kT_set, m + 2)
                for r in range(GRP):
                    b, g = r // 2, r % 2 * 2
                    last = mm(ps_s[:, r * HD:(r + 1) * HD], qT[:, b, g:g + 2, :].rearrange("p g s -> p (g s)"), kT[:, b, :],
                              start=True, stop=True)
                last.then_inc(s_done, 1)

            def project_o(m, wpar, before_last=None):
                pe.wait_ge(oTlo_set, m + 3)
                flat = lambda t, h: t[:, h, :, :].rearrange("p b s -> p (b s)")
                split_product(ps_y[:, :], [(flat(oT_hi, h), flat(oT_lo, h), wo_at(w_hi, wpar, h), wo_at(w_lo, wpar, h))
                                           for h in range(GRP)], before_last).then_inc(y_done, 1)

            pe.wait_ge(s_cst, 16)
            for c in range(CELLS):
                pe.wait_ge(xn_set, c + 1)
                turn_into(first_bank(c, 1), first_xn[c], lat_t)
            pe.wait_ge(first_ctx, 16)
            for c in range(CELLS):
                turn_into(first_bank(c, 0), y[:, CELLS + c, :], ctx_t)
            pe.wait_ge(lat_lo, CELLS)
            with pe.Fori(0, QUARTERS // 2) as j:
                for kpar in range(2):
                    with pe.Fori(0, ITS) as gp:
                        it = (j * 2 + kpar) * ITS + gp
                        pe.wait_ge(ctx_lo, (j * 2 + kpar) * CELLS + CELLS)
                        for s in range(STEPS):
                            i, blk, cell, wpar = it * STEPS + s, it * 2 + s // CELLS, s % CELLS, s // CELLS
                            if cell == 0:
                                pe.wait_ge(w_lo_set, blk * PIECES + 4)
                            pe.wait_ge(q_set, i + 1)
                            project_q(i - 2, kpar, cell, wpar).then_inc(q_done, 1)
                            if cell == 0:
                                pe.wait_ge(w_lo_set, blk * PIECES + 6)
                            pe.wait_ge(vlo_set, i + 1)
                            pe.wait_ge(k_set, i + 1)
                            project_kv(0, kpar, cell, wpar)
                            weigh_v(i - 2, s)
                            if s == 0:
                                pe.wait_ge(ctx_lo, it + CELLS)
                            if s == 6:
                                pe.wait_ge(lat_lo, it + CELLS + 1)
                            if s == 7:
                                pe.wait_ge(ctx_lo, it + CELLS + 1)
                            turn_qk(i - 1, s - 1)
                            project_kv(1, kpar, cell, wpar).then_inc(kv_done, 1)
                            scores(i - 1)
                            if s in (5, 6):
                                turn(it, 6 - s)
                            if cell == 2:
                                pe.wait_ge(w_lo_set, blk * PIECES + PIECES)
                            pe.wait_ge(y_added, i + 1)
                            project_o(i - 2, wpar if cell >= 2 else 1 - wpar)
            pe.wait_ge(q_set, NCELL + 1)
            pe.wait_ge(k_set, NCELL + 1)
            turn_qk(NCELL - 1, 1)
            turn_p(NCELL - 2)
            scores(NCELL - 1)
            weigh_v(NCELL - 2, 0)
            pe.wait_ge(y_added, NCELL + 1)
            project_o(NCELL - 2, 1, before_last=lambda: turn_p(NCELL - 1))
            weigh_v(NCELL - 1, 1)
            pe.wait_ge(y_added, NCELL + 2)
            project_o(NCELL - 1, 1)

            def turn_h(T):
                for c in range(CELLS):
                    pe.wait_ge(f_h, T * CELLS + c + 1)
                    if not isinstance(T, int):
                        pe.wait_ge(f_act, T * (NE * CH) - CH + c + 1)
                    for k in range(CH):
                        last = nc.tensor.transpose(banks[c][:, k * P:(k + 1) * P], h[:, c, k * P:(k + 1) * P], ident)
                    last.then_inc(f_t, 1)

            turn_h(0)
            with pe.Fori(0, QUARTERS) as T:
                def up(e):
                    for k in range(2):
                        pe.wait_ge(f_w_lo[k], (e + 1) * CH // 2)
                    for f in range(CH):
                        k = T * (NE * CH) + e * CH + f
                        if e:
                            pe.wait_ge(f_act, k - CH + 1)
                        at = lambda t, c: t[:, (e * CH + c) * D + f * P:(e * CH + c) * D + (f + 1) * P]
                        split_product(banks[f][:, :], [(at(w1_hi, c), at(w1_lo, c), hT_hi[:, c, :], hT_lo[:, c, :])
                                                       for c in range(CH)]).then_inc(g1_done, 1)
                        if e == 0 and f == 0:
                            strength_sums()

                def strength_sums():
                    pe.wait_ge(f_abs, T * 2 + 2)
                    pe.wait_ge(r_hg, T * (CELLS * NE) + NE + 1)
                    mm(banks[4][:, 0:CELLS], m_text, asum[:, :], start=True, stop=True)
                    mm(banks[4][:, CELLS:2 * CELLS], m_vis, asum[:, :], start=True, stop=True).then_inc(r_sum, 1)

                def down(e):
                    pe.wait_ge(f_alo, T * (NE * CH) + (e + 1) * CH)
                    for c in range(CELLS):
                        if e:
                            pe.wait_ge(f_yadd, T * (NE * CELLS) + (e - 1) * CELLS + c + 1)
                        at = lambda t, f: t[:, (e * CH + f) * D:(e * CH + f + 1) * D]
                        split_product(banks[4 + c][:, :], [
                            (a_hi[:, e % 2, f, c * P:(c + 1) * P], a_lo[:, e % 2, f, c * P:(c + 1) * P], at(w2_hi, f), at(w2_lo, f))
                            for f in range(CH)]).then_inc(g2_done, 1)

                pe.wait_ge(f_tlo, T * CELLS + CELLS)
                up(0)
                pe.wait_ge(r_top, T + 1)
                mm(banks[4][:, 0:2 * CELLS * NE], m_first, pick[:, :, :, :].rearrange("p k c e -> p (k c e)"),
                   start=True, stop=True).then_inc(r_pick, 1)
                up(1)
                pe.wait_ge(r_gate, T + 1)
                pe.wait_ge(w_lo_set, (2 * NIT + 1) * PIECES)
                down(0)
                up(2)
                down(1)
                turn_h(T + 1)
                for k in range(2):
                    pe.wait_ge(f_w_lo[k], FLATE // 2)
                down(2)


_INS = ["x", "ctx_4096", "g_xattn", "g_ffn", "L0_xattn_Wq", "L0_xattn_Wk", "L0_xattn_Wv", "L0_xattn_Wo",
        "L0_xattn_q_norm_w", "L0_xattn_k_norm_w", "L0_ffn_gate_w", "L0_ffn_gate_b", "L0_ffn_w1", "L0_ffn_b1",
        "L0_ffn_w2", "L0_ffn_b2"]


def kernel(**inputs):
    import numpy as np
    import concourse.bacc as bacc
    from concourse.bass_utils import run_bass_kernel_spmd

    n = np.arange(P)
    same = n[:, None] // S == n[None, :] // S
    late = (n[:, None] % S >= VIS)
    consts = np.concatenate([np.eye(P), same & late, same & ~late, same & (n[:, None] % S == 0)], axis=1).astype(np.float32)

    nc = bacc.Bacc("TRN2", target_bir_lowering=False, num_devices=1)
    arrays, args = {}, []
    for name in _INS:
        a = np.ascontiguousarray(inputs[name])
        if name == "L0_ffn_b1":
            a = np.ascontiguousarray(a.reshape(NE * CH, P).T)
        arrays[f"in_{name}"] = a
        args.append(nc.dram_tensor(f"in_{name}", a.shape, mybir.dt.from_np(a.dtype), kind="ExternalInput").ap())
    arrays["consts"] = consts
    args.append(nc.dram_tensor("consts", consts.shape, mybir.dt.float32, kind="ExternalInput").ap())
    args.append(nc.dram_tensor("x2_scratch", (B * S, D), mybir.dt.float32, kind="Internal").ap())
    args.append(nc.dram_tensor("out", (B, S, D), mybir.dt.float32, kind="ExternalOutput").ap())
    flamingo_block(nc, *args)
    r = run_bass_kernel_spmd(nc, [arrays], core_ids=[0])
    return r.results[0]["out"]
```
